# Optimizing a Trainium2 kernel written in Bass

```python
import numpy as np
import jax
import jax.numpy as jnp

def _softmax(x, axis=-1):
    return jax.nn.softmax(x, axis=axis)

def _gelu(x):
    return jax.nn.gelu(x, approximate=True)

def _silu(x):
    return jax.nn.silu(x)

def _sigmoid(x):
    return jax.nn.sigmoid(x)

def _layernorm(x, axis=-1, eps=1e-05):
    m = jnp.mean(x, axis=axis, keepdims=True)
    v = jnp.var(x, axis=axis, keepdims=True)
    return (x - m) / jnp.sqrt(v + eps)

def _scatter_add(tgt, idx, src, axis=0):
    return tgt.at[idx].add(src)

def _segment_sum(src, seg, n):
    return jax.ops.segment_sum(src, seg, n)
kernel_name = 'mk_gnn_resnorm_d1_gnn_r64_3a7596'

def setup_inputs(seed: int=0):
    np.random.seed(seed)
    _w = jnp.asarray

    def _rec_inputs():
        import jax
        import jax.numpy as jnp
        _gk = jax.random.key(seed)
        x = -0.0005121 + 1.001 * jax.random.normal(jax.random.fold_in(_gk, 1), (100000, 32), jnp.float32)
        _s = jax.random.randint(jax.random.fold_in(_gk, 2), (12500,), 0, 100000, jnp.int32)
        _d = jax.random.randint(jax.random.fold_in(_gk, 3), (12500,), 0, 100000, jnp.int32)
        _loop = jnp.arange(100000, dtype=jnp.int32)
        src = jnp.concatenate([_s, _d, _loop])
        dst = jnp.concatenate([_d, _s, _loop])
        _o = jnp.argsort(dst, stable=True)
        src = src[_o]
        dst = dst[_o]
        edge_attr_4 = 0.000398945 + 1.00003 * jax.random.normal(jax.random.fold_in(_gk, 11), (1700000, 4), jnp.float32)
        return (x, src, dst, edge_attr_4)
    x, src, dst, edge_attr_4 = _rec_inputs()

    def _L0_gnn_setup():
        import jax, jax.numpy as jnp
        import numpy as np
        N_NODES = 100000
        N_EDGES = 25000
        IN_DIM = 32
        HID = 64
        OUT_DIM = 32
        EDGE_DIM = 4
        key = jax.random.key(seed)
        ks = jax.random.split(key, 12)
        x = jax.random.normal(ks[0], (N_NODES, IN_DIM), dtype=jnp.float32)
        edge_index = jax.random.randint(ks[1], (2, N_EDGES), 0, N_NODES, dtype=jnp.int32)
        edge_attr = jax.random.normal(ks[2], (N_EDGES, EDGE_DIM), dtype=jnp.float32)

        def lin(k, fan_in, fan_out):
            kw, kb = jax.random.split(k)
            bound = 1.0 / np.sqrt(fan_in)
            W = jax.random.uniform(kw, (fan_in, fan_out), minval=-bound, maxval=bound, dtype=jnp.float32)
            b = jax.random.uniform(kb, (fan_out,), minval=-bound, maxval=bound, dtype=jnp.float32)
            return (W, b)
        W1, b1 = lin(ks[3], 2 * IN_DIM, HID)
        W2, b2 = lin(ks[4], HID, 2 * HID)
        W3, b3 = lin(ks[5], 2 * HID, HID)
        W4, b4 = lin(ks[6], HID, OUT_DIM)
        return {'x': x, 'edge_index': edge_index, 'edge_attr': edge_attr, 'W1': W1, 'b1': b1, 'W2': W2, 'b2': b2, 'W3': W3, 'b3': b3, 'W4': W4, 'b4': b4}
    _L0_gnn_all = _L0_gnn_setup()
    _L0_gnn_in = {k: v for k, v in _L0_gnn_all.items() if k in ('W1', 'b1', 'W2', 'b2', 'W3', 'b3', 'W4', 'b4')}
    del _L0_gnn_all
    return {'x': x, 'src': src, 'dst': dst, 'edge_attr_4': edge_attr_4, 'L0_gnn_W1': _L0_gnn_in['W1'], 'L0_gnn_b1': _L0_gnn_in['b1'], 'L0_gnn_W2': _L0_gnn_in['W2'], 'L0_gnn_b2': _L0_gnn_in['b2'], 'L0_gnn_W3': _L0_gnn_in['W3'], 'L0_gnn_b3': _L0_gnn_in['b3'], 'L0_gnn_W4': _L0_gnn_in['W4'], 'L0_gnn_b4': _L0_gnn_in['b4']}

def reference(x, src, dst, edge_attr_4, L0_gnn_W1, L0_gnn_b1, L0_gnn_W2, L0_gnn_b2, L0_gnn_W3, L0_gnn_b3, L0_gnn_W4, L0_gnn_b4):
    import jax
    import jax.numpy as jnp

    def _L0_gnn_ref(x, edge_index, edge_attr, W1, b1, W2, b2, W3, b3, W4, b4):
        import jax, jax.numpy as jnp
        import numpy as np
        N_NODES = 100000
        N_EDGES = 25000
        IN_DIM = 32
        HID = 64
        OUT_DIM = 32
        EDGE_DIM = 4
        j_idx = edge_index[0]
        i_idx = edge_index[1]
        x_j = x[j_idx]
        x_i = x[i_idx]
        msg = jnp.concatenate([x_i, x_j - x_i], axis=-1)
        h = jax.nn.relu(msg @ W1 + b1)
        h = jax.nn.relu(h @ W2 + b2)
        h = jax.nn.relu(h @ W3 + b3)
        m = h @ W4 + b4
        s = jax.ops.segment_sum(m, i_idx, num_segments=N_NODES)
        cnt = jax.ops.segment_sum(jnp.ones((m.shape[0],), m.dtype), i_idx, num_segments=N_NODES)
        return s / jnp.maximum(cnt, 1.0)[:, None]
    edge_index = jnp.stack([src, dst])
    x = _layernorm(x + _L0_gnn_ref(x, edge_index, edge_attr_4, L0_gnn_W1, L0_gnn_b1, L0_gnn_W2, L0_gnn_b2, L0_gnn_W3, L0_gnn_b3, L0_gnn_W4, L0_gnn_b4), axis=-1)
    return x

_drawn_inputs = setup_inputs


def setup_inputs(seed=0):
    import zlib

    import numpy as np

    out = dict(_drawn_inputs(seed))
    spreads = {}
    factors = {'L0_gnn_W1': 3.404, 'L0_gnn_b1': 8.0, 'L0_gnn_W2': 2.729, 'L0_gnn_b2': 4.996}
    for name, (base, spread) in spreads.items():
        noise = np.random.default_rng([zlib.crc32(name.encode()), seed]).standard_normal(out[name].shape)
        drawn = base * np.exp(spread * noise) if base else spread * noise
        out[name] = jnp.asarray(drawn.astype(out[name].dtype))
    for name, factor in factors.items():
        out[name] = (out[name] * factor).astype(out[name].dtype)
    return out
```

```python
import concourse.bass as bass
from concourse import mybir
from contextlib import ExitStack

F32 = mybir.dt.float32
I32 = mybir.dt.int32
ALU = mybir.AluOpType
ACT = mybir.ActivationFunctionType
AX = mybir.AxisListType

P = 128
EPS = 1e-5
NOWHERE = 1 << 20
SRC_BITS = 17
TOP = 8


def wait(eng, sem, value):
    if isinstance(value, int) and value <= 0:
        return
    eng.wait_ge(sem, value)


class Count:

    def __init__(self, eng, sem):
        self.eng, self.sem, self.n = eng, sem, 0
        self.built = 0

    def up(self, instruction):
        instruction.then_inc(self.sem, 1)
        self.n = self.n + 1
        self.built += 1

    def settle(self):
        wait(self.eng, self.sem, self.n)


def gnn_program(nc, x, src, dst, W1, b1, W2, b2, W3, b3, W4, b4, out):
    N, D = x.shape
    E = src.shape[0]
    H1, H2, H3 = W1.shape[1], W2.shape[1], W3.shape[1]
    ROW = D + 1
    assert (2 * D, H1, H2, H3, W4.shape[1]) == (64, 64, 128, 64, 32) and N < 1 << SRC_BITS

    EDGE_COLS = -(-E // P)
    LAST_COLS = E - (P - 1) * EDGE_COLS
    SLOTS = 240
    BATCHES = SLOTS // TOP
    CHAIN_STEPS = 2 * (10 + 12)
    MERGE_STEPS = 2 + 5
    LAST_STEPS = 2 * (3 + 2)
    PAIR_MARKS, TILE_MARKS = 2 * 3, 4
    KEY_TOP = 2048 + EDGE_COLS

    NPP = 16
    BLOCK = P * NPP
    FULL = N // BLOCK
    REST = (N - FULL * BLOCK) // NPP
    BLOCKS = FULL + 1
    assert 0 < REST < P and (N - FULL * BLOCK) % NPP == 0 and FULL % 2 == 0

    HALF_TURN = "ABABXABX"
    HALF_LEN, HALF_BLOCKS, HALF_TILES = len(HALF_TURN), 3, 5
    PATTERN = HALF_TURN * 2
    LEN = len(PATTERN)
    TURNS = BATCHES // 4
    UNITS = PATTERN * TURNS + HALF_TURN + "AB" * (BLOCKS - HALF_BLOCKS * (2 * TURNS + 1))
    assert BATCHES == 4 * TURNS + 2 and UNITS.count("A") == BLOCKS and UNITS.count("X") == BATCHES
    RING = HALF_BLOCKS
    TILE_OF = [sum(k != "B" for k in UNITS[:u + 1]) - 1 for u in range(len(UNITS))]
    NUMBER_OF = [UNITS[:u + 1].count("X" if UNITS[u] == "X" else "A") - 1 for u in range(len(UNITS))]
    TILE_OF_BLOCK = [TILE_OF[u] for u in range(len(UNITS)) if UNITS[u] == "A"]
    FREE_AT = [max([v + 1 for v in range(len(UNITS)) if TILE_OF[v] == TILE_OF[u] - 2], default=0)
               for u in range(len(UNITS))]
    PER_TURN = {"unit": LEN, "tile": 2 * HALF_TILES, "A": 2 * HALF_BLOCKS, "X": 4}

    def exists(turn, pos):
        return not isinstance(turn, int) or 0 <= turn * LEN + pos < len(UNITS)

    def kind(turn, pos):
        return UNITS[turn * LEN + pos] if isinstance(turn, int) else UNITS[LEN + pos]

    def at(turn, pos, numbers, step):
        if isinstance(turn, int):
            return numbers[turn * LEN + pos]
        return (turn - 1) * step + numbers[LEN + pos]

    def tile_of(turn, pos):
        return at(turn, pos, TILE_OF, PER_TURN["tile"])

    def number_of(turn, pos):
        return at(turn, pos, NUMBER_OF, PER_TURN["X" if kind(turn, pos) == "X" else "A"])

    def place_of(turn, pos, numbers, ring):
        return numbers[turn * LEN + pos if isinstance(turn, int) else LEN + pos] % ring

    def run_steps(eng, step, prologue):
        prologue()
        for pos in range(LEN):
            step(0, pos)
        with eng.Fori(1, TURNS) as turn:
            for pos in range(LEN):
                step(turn, pos)
        for pos in range(len(UNITS) - TURNS * LEN + 3):
            step(TURNS, pos)

    table = nc.dram_tensor("sums_of_messages", (N, ROW), F32).ap()
    x_blocks = x[0:FULL * BLOCK, :].rearrange("(b p c) f -> b p (c f)", p=P, c=NPP)
    x_rest = x[FULL * BLOCK:N, :].rearrange("(p c) f -> p (c f)", c=NPP)
    out_blocks = out[0:FULL * BLOCK, :].rearrange("(b p c) f -> b p (c f)", p=P, c=NPP)
    out_rest = out[FULL * BLOCK:N, :].rearrange("(p c) f -> p (c f)", c=NPP)
    table_blocks = table[0:FULL * BLOCK, :].rearrange("(b p c) f -> b p (c f)", p=P, c=NPP)
    table_rest = table[FULL * BLOCK:N, :].rearrange("(p c) f -> p (c f)", c=NPP)

    with ExitStack() as ctx:
        def sb(name, shape, dt=F32):
            return ctx.enter_context(nc.sbuf_tensor(name, shape, dt))

        def sem(name):
            return ctx.enter_context(nc.semaphore(name))

        src_sb = sb("src_sb", [P, EDGE_COLS], I32)
        dst_sb = sb("dst_sb", [P, EDGE_COLS], I32)
        nxt_sb = sb("nxt_sb", [P, EDGE_COLS], I32)
        key = sb("key", [P, EDGE_COLS], I32)
        key_f = key[:, :].bitcast(F32)
        work_a = sb("work_a", [P, EDGE_COLS])
        work_b = sb("work_b", [P, EDGE_COLS])
        extra = sb("extra", [P, EDGE_COLS])
        countdown = sb("countdown", [P, EDGE_COLS], I32)
        self_msg = sb("self_msg", [P, BLOCKS, NPP * D])

        ident = sb("ident", [P, P])
        ones = sb("ones", [P, P])
        before = sb("before", [P, P])
        earlier = sb("earlier", [P, P])
        w1_pair = sb("w1_pair", [P, P])
        w1_self = sb("w1_self", [P, P])
        w2_twice = sb("w2_twice", [P, P])
        w3_sb = sb("w3_sb", [P, H3])
        w4_pair = sb("w4_pair", [P, 2 * D])
        b1_sb = sb("b1_sb", [P, 1])
        b2_sb = sb("b2_sb", [P, 1])
        b3_sb = sb("b3_sb", [P, 1])
        base_row = sb("base_row", [P, ROW])
        base_tile = sb("base_tile", [P, NPP, ROW])

        stats = sb("stats", [P, 3])
        largest_fall = sb("largest_fall", [P, 1])
        extras_in_row = sb("extras_in_row", [P, 1])
        checks = sb("checks", [P, 3])
        flag_f = sb("flag_f", [P, 1])
        flag = sb("flag", [P, 1], I32)
        row_start = sb("row_start", [P, 1])
        node_base = sb("node_base", [P, 1])
        minus_slot = sb("minus_slot", [P, SLOTS])
        slot_base = sb("slot_base", [P, SLOTS])

        top = sb("top", [P, TOP])
        top_bits = top[:, :].bitcast(I32)
        mark = sb("mark", [P, 1])
        pool_mark = sb("pool_mark", [P, 1])
        key_count = sb("key_count", [P, TOP], I32)
        found = sb("found", [P, TOP])
        slot_dst = sb("slot_dst", [P, TOP])
        dst_of_slot = sb("dst_of_slot", [P, SLOTS + 2])
        src_index = sb("src_index", [P, 2, TOP], I32)
        dst_index = sb("dst_index", [P, 2, TOP], I32)
        out_index = sb("out_index", [P, 2, TOP], I32)
        gathered = sb("gathered", [P, 2, TOP, 2 * D])
        x_in = sb("x_in", [P, RING, NPP * D])
        xT = sb("xT", [P, 2, 512])
        h1 = sb("h1", [P, 2, 512])
        h2 = sb("h2", [P, 2, 2, 512])
        h3 = sb("h3", [P, 2, 512])
        msg = sb("msg", [P, ROW, TOP + 1])
        same_run = sb("same_run", [P, ROW, TOP + 1])
        run_sum = sb("run_sum", [P, ROW, TOP + 1])
        first_part = sb("first_part", [P, ROW, TOP])
        first_add = sb("first_add", [P, ROW])
        first_sum = sb("first_sum", [P, ROW])
        is_first = sb("is_first", [P, TOP])
        run_end = sb("run_end", [P, TOP])
        not_first = sb("not_first", [P, TOP])
        rows_out = sb("rows_out", [P, 2, TOP, ROW])

        merge_dst = sb("merge_dst", [P, 1])
        merge_index = sb("merge_index", [P, 1], I32)
        merge_out = sb("merge_out", [P, 1], I32)
        merge_src = sb("merge_src", [P, 1], I32)
        dst_diag = sb("dst_diag", [P, P])
        equal = sb("equal", [P, P])
        equal_earlier = sb("equal_earlier", [P, P])
        repeats = sb("repeats", [P, 1])
        shifted = sb("shifted", [P, 1])
        first_of = sb("first_of", [P, 1])
        table_rows = sb("table_rows", [P, ROW])
        new_rows = sb("new_rows", [P, ROW])
        tile_msg = sb("tile_msg", [P, ROW])
        tile_x = sb("tile_x", [P, 4 * D])

        x_last = sb("x_last", [P, 2, NPP, D])
        sums = sb("sums", [P, 2, NPP, ROW])
        counts = sb("counts", [P, 2, NPP])
        share = sb("share", [P, 2, NPP])
        mean_msg = sb("mean_msg", [P, 2, NPP, D])
        y = work_a[:, 0:NPP * D].rearrange("p (c f) -> p c f", f=D)
        y_sum = sb("y_sum", [P, NPP])
        y_mean = sb("y_mean", [P, NPP])
        centred = sb("centred", [P, 2, NPP, D])
        square = sb("square", [P, 2, NPP, D])
        y_var = sb("y_var", [P, NPP])
        var = sb("var", [P, 2, NPP])
        std = sb("std", [P, 2, NPP])
        rstd = sb("rstd", [P, NPP])
        result = sb("result", [P, 2, NPP, D])

        def bank(name):
            return ctx.enter_context(nc.psum_tensor(name, [P, 512], F32))

        t_ps = [bank("t_ps0"), bank("t_ps1")]
        h1_ps, h2a_ps, h2b_ps, h3_ps = bank("h1_ps"), bank("h2a_ps"), bank("h2b_ps"), bank("h3_ps")
        self_ps, extra_ps = bank("self_ps"), bank("extra_ps")
        h2_ps = [h2a_ps, h2b_ps]

        pads_set = sem("pads_set")
        edges_in = sem("edges_in")
        zeros_set = sem("zeros_set")
        dve_set = sem("dve_set")
        weights_in = sem("weights_in")
        consts_set = sem("consts_set")
        pool_steps = sem("pool_steps")
        pool_marks = sem("pool_marks")
        dve_steps = sem("dve_steps")
        dve_last_steps = sem("dve_last_steps")
        stats_ready = sem("stats_ready")
        totals_ready = sem("totals_ready")
        flag_ready = sem("flag_ready")
        table_started = sem("table_started")
        base_ready = sem("base_ready")

        x_loaded = [sem(f"x_loaded{i}") for i in range(RING)]
        slots_found = sem("slots_found")
        batch_gathered = [sem(f"batch_gathered{i}") for i in range(2)]
        difference_ready = sem("difference_ready")
        transposed = sem("transposed")
        xT_ready = sem("xT_ready")
        h1_done, h1_ready = sem("h1_done"), sem("h1_ready")
        h2_done, h2_ready = sem("h2_done"), sem("h2_ready")
        h3_done, h3_ready = sem("h3_done"), sem("h3_ready")
        msg_done = sem("msg_done")
        self_stored = sem("self_stored")
        extras_taken = sem("extras_taken")
        rows_ready = sem("rows_ready")
        rows_stored = [sem(f"rows_stored{i}") for i in range(2)]

        merge_asked = sem("merge_asked")
        diag_ready = sem("diag_ready")
        dst_spread = sem("dst_spread")
        equal_ready = sem("equal_ready")
        merged = sem("merged")
        merge_gathered = sem("merge_gathered")
        merge_rows_ready = sem("merge_rows_ready")
        merge_stored = sem("merge_stored")
        tile_gathered = sem("tile_gathered")
        tile_diff = sem("tile_diff")
        tile_pe = sem("tile_pe")
        tile_act = sem("tile_act")
        tile_msg_ready = sem("tile_msg_ready")

        table_done = sem("table_done")
        self_done = sem("self_done")
        last_loaded = [sem(f"last_loaded{i}") for i in range(2)]
        mean_ready = sem("mean_ready")
        mean_added = sem("mean_added")
        share_ready = sem("share_ready")
        y_ready = sem("y_ready")
        centred_ready = sem("centred_ready")
        square_ready = sem("square_ready")
        var_ready = sem("var_ready")
        std_ready = sem("std_ready")
        result_ready = sem("result_ready")
        result_stored = [sem(f"result_stored{i}") for i in range(2)]

        WEIGHT_LOADS = 18
        EDGE_LOADS = 9
        SPLIT = (P - 1) // 16 * 16

        def take_way(eng):
            eng.wait_ge(flag_ready, 1)
            return eng.value_load(flag[0:1, 0:1], min_val=0, max_val=1)

        block = ctx.enter_context(nc.Block())

        @block.sync
        def _(sp):
            sp.wait_ge(pads_set, 3)
            for tile, flat, n in ((dst_sb, dst, E), (nxt_sb, dst[1:E], E - 1), (src_sb, src, E)):
                for lo, hi in ((0, SPLIT), (SPLIT, P - 1)):
                    sp.dma_start(tile[lo:hi, :], flat[lo * EDGE_COLS:hi * EDGE_COLS].rearrange(
                        "(p c) -> p c", c=EDGE_COLS)).then_inc(edges_in, 16)
                cols = n - (P - 1) * EDGE_COLS
                sp.dma_start(tile[P - 1:P, 0:cols], flat[(P - 1) * EDGE_COLS:n].rearrange(
                    "(p c) -> p c", p=1)).then_inc(edges_in, 16)

            way = take_way(sp)
            with sp.If(way == 1):
                def load_block(b, ring, tiles):
                    wait(sp, transposed, tiles)
                    sp.dma_start(x_in[:, ring, :], x_blocks[b]).then_inc(x_loaded[ring], 16)

                for b in range(RING):
                    load_block(b, b, 0)
                with sp.Fori(1, 2 * TURNS + 1) as half:
                    for r in range(RING):
                        load_block(half * RING + r, r, (half - 1) * HALF_TILES + TILE_OF_BLOCK[r] + 1)
                for b in range((2 * TURNS + 1) * RING, FULL):
                    load_block(b, b % RING, TILE_OF_BLOCK[b - RING] + 1)
                wait(sp, transposed, TILE_OF_BLOCK[FULL - RING] + 1)
                sp.dma_start(x_in[0:REST, FULL % RING, :], x_rest).then_inc(x_loaded[FULL % RING], 16)

            sp.wait_ge(table_done, 1)

            def load_last(b, i, used):
                wait(sp, mean_ready, used)
                wait(sp, y_ready, used)
                sp.dma_start(x_last[:, i, :, :], x_blocks[b]).then_inc(last_loaded[i], 16)
                sp.dma_start(sums[:, i, :, :], table_blocks[b]).then_inc(last_loaded[i], 16)

            def store_last(b, i, made):
                sp.wait_ge(result_ready, made)
                sp.dma_start(out_blocks[b], result[:, i, :, :]).then_inc(result_stored[i], 16)

            load_last(0, 0, 0)
            load_last(1, 1, 0)
            with sp.Fori(0, FULL // 2 - 1) as pair:
                for i in range(2):
                    load_last(pair * 2 + 2 + i, i, pair * 2 + i + 1)
                    store_last(pair * 2 + i, i, pair * 2 + i + 1)
            wait(sp, mean_ready, FULL - 1)
            wait(sp, y_ready, FULL - 1)
            sp.dma_start(x_last[0:REST, 0, :, :], x_rest).then_inc(last_loaded[0], 16)
            sp.dma_start(sums[0:REST, 0, :, :], table_rest).then_inc(last_loaded[0], 16)
            store_last(FULL - 2, 0, FULL - 1)
            store_last(FULL - 1, 1, FULL)
            sp.wait_ge(result_ready, BLOCKS)
            sp.dma_start(out_rest, result[0:REST, 0, :, :]).then_inc(result_stored[0], 16)
            sp.wait_ge(result_stored[0], 16 * (FULL // 2 + 1))
            sp.wait_ge(result_stored[1], 16 * (FULL // 2))

        @block.scalar
        def _(act):
            act.wait_ge(zeros_set, 5)

            def column(v):
                return v.rearrange("(n a) -> n a", a=1)

            loads = []
            for h in (0, 1):
                loads += [(w1_pair[64 * h:64 * h + 64, 64 * h:64 * h + 64], W1),
                          (w2_twice[64 * h:64 * h + 64, :], W2),
                          (w4_pair[64 * h:64 * h + 64, D * h:D * h + D], W4),
                          (b1_sb[64 * h:64 * h + 64, :], column(b1)),
                          (b3_sb[64 * h:64 * h + 64, :], column(b3))]
            for q in range(4):
                loads.append((w1_self[D * q:D * q + D, 64 * (q % 2):64 * (q % 2) + 64], W1[0:D, :]))
            loads += [(w3_sb[:, :], W3), (b2_sb[:, :], column(b2)),
                      (base_row[:, 0:D], b4.rearrange("(a n) -> a n", a=1).to_broadcast([P, D]))]
            assert len(loads) == WEIGHT_LOADS - 1
            for place, what in loads:
                act.dma_start(place, what).then_inc(weights_in, 16)

            act.wait_ge(base_ready, 1)
            act.dma_start(table_blocks.rearrange("b p n -> p b n"),
                          base_tile[:, :, :].rearrange("p c f -> p (c f)").unsqueeze(1).to_broadcast([P, FULL, NPP * ROW])
                          ).then_inc(table_started, 16)
            act.dma_start(table_rest, base_tile[0:REST, :, :].rearrange("p c f -> p (c f)")).then_inc(table_started, 16)

            way = take_way(act)
            with act.If(way == 1):
                act.wait_ge(weights_in, 16 * (WEIGHT_LOADS - 1))

                def act_step(turn, pos):
                    u = turn * LEN + pos
                    if exists(turn, pos + 1) and kind(turn, pos + 1) != "B":
                        par = place_of(turn, pos + 1, TILE_OF, 2)
                        act.wait_ge(transposed, tile_of(turn, pos + 1) + 1)
                        wait(act, h1_done, at(turn, pos + 1, FREE_AT, LEN))
                        act.activation(xT[:, par, :], t_ps[par][:, :], ACT.Copy).then_inc(xT_ready, 1)
                    if exists(turn, pos):
                        act.wait_ge(h1_done, u + 1)
                        wait(act, h2_done, (u - 1) * 2)
                        act.activation(h1[:, pos % 2, :], h1_ps[:, :], ACT.Relu, bias=b1_sb[:, 0:1]).then_inc(h1_ready, 1)
                    if exists(turn, pos - 1):
                        for j in range(2):
                            act.wait_ge(h2_done, (u - 1) * 2 + j + 1)
                            wait(act, h3_done, (u - 2) * 2)
                            act.activation(h2[:, (pos - 1) % 2, j, :], h2_ps[j][:, :], ACT.Relu,
                                           bias=b2_sb[:, 0:1]).then_inc(h2_ready, 1)
                    if exists(turn, pos - 2):
                        act.wait_ge(h3_done, (u - 1) * 2)
                        wait(act, msg_done, u - 3)
                        act.activation(h3[:, (pos - 2) % 2, :], h3_ps[:, :], ACT.Relu, bias=b3_sb[:, 0:1]).then_inc(h3_ready, 1)
                    if exists(turn, pos - 3) and kind(turn, pos - 3) != "X":
                        half = "AB".index(kind(turn, pos - 3))
                        act.wait_ge(msg_done, u - 2)
                        place = self_msg[:, bass.ds(number_of(turn, pos - 3), 1), :].rearrange(
                            "p b (k h n) -> p (b k) h n", k=4, h=2)
                        act.activation(place[:, :, half, :], self_ps[:, 0:256].rearrange("p (k n) -> p k n", k=4),
                                       ACT.Copy).then_inc(self_stored, 1)

                def first_tile():
                    act.wait_ge(transposed, 1)
                    act.activation(xT[:, 0, :], t_ps[0][:, :], ACT.Copy).then_inc(xT_ready, 1)

                run_steps(act, act_step, first_tile)
                act.drain().then_inc(self_done, 1)
            with act.If(way == 0):
                act.wait_ge(weights_in, 16 * (WEIGHT_LOADS - 1))
                def act_tile(t):
                    act.wait_ge(tile_pe, t * 7 + 1)
                    act.activation(xT[:, 0, 0:P], t_ps[0][:, 0:P], ACT.Copy).then_inc(tile_act, 1)
                    act.wait_ge(tile_pe, t * 7 + 2)
                    act.activation(h1[:, 0, 0:P], h1_ps[:, 0:P], ACT.Relu, bias=b1_sb[:, 0:1]).then_inc(tile_act, 1)
                    for j in range(2):
                        act.wait_ge(tile_pe, t * 7 + 3 + j)
                        act.activation(h2[:, 0, j, 0:P], h2_ps[j][:, 0:P], ACT.Relu, bias=b2_sb[:, 0:1]).then_inc(tile_act, 1)
                    act.wait_ge(tile_pe, t * 7 + 6)
                    act.activation(h3[:, 0, 0:P], h3_ps[:, 0:P], ACT.Relu, bias=b3_sb[:, 0:1]).then_inc(tile_act, 1)

                act_tile(0)
                with act.Fori(1, EDGE_COLS) as t:
                    act_tile(t)

            def act_last(number, i):
                act.wait_ge(centred_ready, number + 1)
                wait(act, var_ready, number - 1)
                act.activation(square[:, i, :, :], centred[:, i, :, :], ACT.Square).then_inc(square_ready, 1)
                act.wait_ge(var_ready, number + 1)
                wait(act, result_ready, number - 1)
                act.activation(std[:, i, :], var[:, i, :], ACT.Sqrt).then_inc(std_ready, 1)

            act_last(0, 0)
            act_last(1, 1)
            with act.Fori(1, FULL // 2) as pair:
                for i in range(2):
                    act_last(pair * 2 + i, i)
            act_last(FULL, 0)

        @block.tensor
        def _(pe):
            pe.wait_ge(consts_set, 4)
            pe.wait_ge(stats_ready, 1)
            pe.matmul(extra_ps[:, 0:3], ones[:, :], stats[:, :], start=True, stop=True)
            pe.matmul(extra_ps[:, 4:5], before[:, :], extras_in_row[:, :], start=True, stop=True).then_inc(totals_ready, 1)

            def merge(number):
                pe.wait_ge(diag_ready, number)
                pe.matmul(t_ps[1][:, 0:P], ones[:, :], dst_diag[:, :], start=True, stop=True).then_inc(dst_spread, 1)
                pe.wait_ge(equal_ready, number)

            way = take_way(pe)
            with pe.If(way == 1):
                pe.wait_ge(weights_in, 16 * (WEIGHT_LOADS - 1))

                def transposes(turn, pos):
                    par = place_of(turn, pos, TILE_OF, 2)
                    wait(pe, xT_ready, tile_of(turn, pos) - 1)
                    if kind(turn, pos) == "X":
                        buf = place_of(turn, pos, NUMBER_OF, 2)
                        pe.wait_ge(difference_ready, number_of(turn, pos) + 1)
                        tile = gathered[:, buf, :, :].rearrange("p s f -> p (s f)")
                    else:
                        ring = place_of(turn, pos, NUMBER_OF, RING)
                        rounds = at(turn, pos, [n // RING for n in NUMBER_OF], 2)
                        pe.wait_ge(x_loaded[ring], rounds * 16 + 16)
                        tile = x_in[:, ring, :]
                    for j in range(4):
                        last = pe.transpose(t_ps[par][:, j * P:(j + 1) * P], tile[:, j * P:(j + 1) * P], ident[:, :])
                    last.then_inc(transposed, 1)

                def pe_step(turn, pos):
                    u = turn * LEN + pos
                    if exists(turn, pos + 1) and kind(turn, pos + 1) != "B":
                        transposes(turn, pos + 1)
                    if exists(turn, pos):
                        k, par = kind(turn, pos), place_of(turn, pos, TILE_OF, 2)
                        pe.wait_ge(xT_ready, tile_of(turn, pos) + 1)
                        wait(pe, h1_ready, u)
                        lo, hi = {"A": (0, 64), "B": (64, P), "X": (0, P)}[k]
                        w = w1_pair if k == "X" else w1_self
                        pe.matmul(h1_ps[:, :], w[lo:hi, :], xT[lo:hi, par, :], start=True, stop=True).then_inc(h1_done, 1)
                    if exists(turn, pos - 1):
                        pe.wait_ge(h1_ready, u)
                        for j in range(2):
                            wait(pe, h2_ready, (u - 2) * 2 + j + 1)
                            pe.matmul(h2_ps[j][:, :], w2_twice[64 * j:64 * j + 64, :],
                                      h1[64 * j:64 * j + 64, (pos - 1) % 2, :], start=True, stop=True).then_inc(h2_done, 1)
                    if exists(turn, pos - 2):
                        wait(pe, h3_ready, u - 2)
                        for j in range(2):
                            pe.wait_ge(h2_ready, (u - 2) * 2 + j + 1)
                            pe.matmul(h3_ps[64 * j:64 * j + 64, :], w3_sb[:, :], h2[:, (pos - 2) % 2, j, :],
                                      start=True, stop=True).then_inc(h3_done, 1)
                    if exists(turn, pos - 3):
                        k, number = kind(turn, pos - 3), number_of(turn, pos - 3)
                        pe.wait_ge(h3_ready, u - 2)
                        if k == "X":
                            wait(pe, extras_taken, number)
                        else:
                            wait(pe, self_stored, number * 2 + "AB".index(k))
                        place = extra_ps if k == "X" else self_ps
                        for j in range(4):
                            last = pe.matmul(place[:, 64 * j:64 * j + 64], h3[:, (pos - 3) % 2, j * P:(j + 1) * P],
                                             w4_pair[:, :], start=True, stop=True)
                        last.then_inc(msg_done, 1)

                run_steps(pe, pe_step, lambda: transposes(0, 0))
                merge(1)
                pe.matmul(extra_ps[:, 256:256 + ROW], equal[:, :], first_sum[:, :], start=True, stop=True).then_inc(merged, 1)

            with pe.If(way == 0):
                pe.wait_ge(weights_in, 16 * (WEIGHT_LOADS - 1))
                def pe_tile(t):
                    pe.wait_ge(tile_diff, t + 1)
                    pe.transpose(t_ps[0][:, 0:P], tile_x[:, :], ident[:, :]).then_inc(tile_pe, 1)
                    pe.wait_ge(tile_act, t * 5 + 1)
                    pe.matmul(h1_ps[:, 0:P], w1_pair[:, :], xT[:, 0, 0:P], start=True, stop=True).then_inc(tile_pe, 1)
                    pe.wait_ge(tile_act, t * 5 + 2)
                    for j in range(2):
                        pe.matmul(h2_ps[j][:, 0:P], w2_twice[64 * j:64 * j + 64, :], h1[64 * j:64 * j + 64, 0, 0:P],
                                  start=True, stop=True).then_inc(tile_pe, 1)
                    for j in range(2):
                        pe.wait_ge(tile_act, t * 5 + 3 + j)
                        pe.matmul(h3_ps[64 * j:64 * j + 64, 0:P], w3_sb[:, :], h2[:, 0, j, 0:P],
                                  start=True, stop=True).then_inc(tile_pe, 1)
                    pe.wait_ge(tile_act, t * 5 + 5)
                    pe.matmul(extra_ps[:, 0:64], h3[:, 0, 0:P], w4_pair[:, :], start=True, stop=True).then_inc(tile_pe, 1)
                    merge(t + 1)
                    pe.wait_ge(tile_msg_ready, t + 1)
                    pe.matmul(self_ps[:, 0:ROW], equal[:, :], tile_msg[:, :], start=True, stop=True).then_inc(merged, 1)

                pe_tile(0)
                with pe.Fori(1, EDGE_COLS) as t:
                    pe_tile(t)

        @block.gpsimd
        def _(pool):
            steps = Count(pool, pool_steps)
            pool.memset(w1_pair[:, :], 0.0).then_inc(zeros_set, 1)
            pool.memset(w1_self[:, :], 0.0).then_inc(zeros_set, 1)
            pool.memset(w4_pair[:, :], 0.0).then_inc(zeros_set, 1)
            pool.memset(base_row[:, :], 1.0).then_inc(zeros_set, 1)
            pool.iota(countdown[:, :], [[-1, EDGE_COLS]], base=KEY_TOP, channel_multiplier=0).then_inc(consts_set, 1)
            pool.iota(row_start[:, :], [[0, 1]], base=KEY_TOP, channel_multiplier=EDGE_COLS,
                      allow_small_or_imprecise_dtypes=True).then_inc(zeros_set, 1)
            pool.iota(minus_slot[:, :], [[-1, SLOTS]], base=0, channel_multiplier=0,
                      allow_small_or_imprecise_dtypes=True).then_inc(consts_set, 1)
            steps.up(pool.memset(ident[:, :], 0.0))
            steps.up(pool.memset(ones[:, :], 1.0))
            steps.settle()
            pool.affine_select(out=ident[:, :], in_=ident[:, :], compare_op=ALU.not_equal, fill=1.0, base=0,
                               pattern=[[-1, P]], channel_multiplier=1).then_inc(consts_set, 1)
            steps.up(pool.affine_select(out=before[:, :], in_=ones[:, :], compare_op=ALU.is_gt, fill=0.0, base=0,
                                        pattern=[[1, P]], channel_multiplier=-1))
            steps.up(pool.affine_select(out=earlier[:, :], in_=ones[:, :], compare_op=ALU.is_gt, fill=0.0, base=0,
                                        pattern=[[-1, P]], channel_multiplier=1))
            steps.settle()
            pool.drain().then_inc(consts_set, 1)

            marks = Count(pool, pool_marks)

            def hold(semaphore, value):
                if isinstance(value, int) and value <= 0:
                    return
                pool.wait_ge(semaphore, value)
                marks.settle()
                marks.up(pool.tensor_tensor(pool_mark[:, :], ones[:, 0:1], ones[:, 0:1], ALU.add))

            def merge_gather(number):
                hold(merge_asked, number)
                pool.indirect_dma_start(table_rows[:, :], None, table[:, :],
                                        bass.IndirectOffsetOnAxis(merge_index[:, 0:1], 0)).then_inc(merge_gathered, 16)

            def merge_scatter(number):
                hold(merge_rows_ready, number)
                pool.indirect_dma_start(table[:, :], bass.IndirectOffsetOnAxis(merge_out[:, 0:1], 0), new_rows[:, :], None,
                                        bounds_check=N - 1, oob_is_err=False).then_inc(merge_stored, 16)

            marks_before = marks.n
            way = take_way(pool)
            with pool.If(way == 1):
                def gather(pair, buf):
                    hold(slots_found, pair * 2 + buf + 1)
                    hold(transposed, (pair - 1) * HALF_TILES + 2 + 2 * buf + 1)
                    for s in range(TOP):
                        pool.indirect_dma_start(gathered[:, buf, s, 0:D], None, x[:, :],
                                                bass.IndirectOffsetOnAxis(dst_index[:, buf, s:s + 1], 0)
                                                ).then_inc(batch_gathered[buf], 16)
                        pool.indirect_dma_start(gathered[:, buf, s, D:2 * D], None, x[:, :],
                                                bass.IndirectOffsetOnAxis(src_index[:, buf, s:s + 1], 0)
                                                ).then_inc(batch_gathered[buf], 16)

                def scatter(pair, buf):
                    hold(rows_ready, pair * 2 + buf + 1)
                    for s in range(TOP):
                        pool.indirect_dma_start(table[:, :], bass.IndirectOffsetOnAxis(out_index[:, buf, s:s + 1], 0),
                                                rows_out[:, buf, s, :], None, bounds_check=N - 1,
                                                oob_is_err=False).then_inc(rows_stored[buf], 16)

                gather(0, 0)
                gather(0, 1)
                hold(table_started, 32)
                start, built = marks.n, marks.built
                with pool.Fori(1, BATCHES // 2) as pair:
                    marks.n = (pair - 1) * PAIR_MARKS + start
                    for i in range(2):
                        gather(pair, i)
                        scatter(pair - 1, i)
                assert marks.built == built + PAIR_MARKS
                marks.n = start + (BATCHES // 2 - 1) * PAIR_MARKS
                scatter(BATCHES // 2 - 1, 0)
                scatter(BATCHES // 2 - 1, 1)
                hold(rows_stored[0], 16 * TOP * (BATCHES // 2))
                hold(rows_stored[1], 16 * TOP * (BATCHES // 2))
                merge_gather(1)
                merge_scatter(1)
                hold(merge_stored, 16)
                pool.drain().then_inc(table_done, 1)
            with pool.If(way == 0):
                marks.n = marks_before
                pool.memset(self_msg[:, :, :], 0.0).then_inc(self_done, 1)
                hold(table_started, 32)
                def pool_tile(t):
                    hold(merge_asked, t + 1)
                    pool.indirect_dma_start(tile_x[:, 0:D], None, x[:, :],
                                            bass.IndirectOffsetOnAxis(merge_index[:, 0:1], 0)).then_inc(tile_gathered, 16)
                    pool.indirect_dma_start(tile_x[:, D:2 * D], None, x[:, :],
                                            bass.IndirectOffsetOnAxis(merge_src[:, 0:1], 0)).then_inc(tile_gathered, 16)
                    hold(merge_stored, t * 16)
                    merge_gather(t + 1)
                    merge_scatter(t + 1)

                pool_tile(0)
                start, built = marks.n, marks.built
                with pool.Fori(1, EDGE_COLS) as t:
                    marks.n = (t - 1) * TILE_MARKS + start
                    pool_tile(t)
                assert marks.built == built + TILE_MARKS
                marks.n = start + (EDGE_COLS - 1) * TILE_MARKS
                hold(merge_stored, 16 * EDGE_COLS)
                pool.drain().then_inc(table_done, 1)

            pool.wait_ge(self_done, 1)

            def pool_last(b, i, round_):
                pool.wait_ge(last_loaded[i], round_ * 32 + 32)
                wait(pool, y_ready, b - 1)
                pool.tensor_tensor(mean_msg[:, i, :, :], sums[:, i, :, 0:D],
                                   self_msg[:, bass.ds(b, 1), :].rearrange("p b (c f) -> p (b c) f", f=D),
                                   ALU.add).then_inc(mean_added, 1)
                pool.wait_ge(share_ready, b + 1)
                pool.wait_ge(mean_added, b + 1)
                pool.tensor_tensor(mean_msg[:, i, :, :], mean_msg[:, i, :, :],
                                   share[:, i, :].unsqueeze(2).to_broadcast([P, NPP, D]), ALU.mult).then_inc(mean_ready, 1)

            pool_last(0, 0, 0)
            pool_last(1, 1, 0)
            with pool.Fori(1, FULL // 2) as pair:
                for i in range(2):
                    pool_last(pair * 2 + i, i, pair)
            pool_last(FULL, 0, FULL // 2)

        @block.vector
        def _(dve):
            steps = Count(dve, dve_steps)
            last_steps = Count(dve, dve_last_steps)

            def merge_start(column, number):
                dve.tensor_scalar(merge_index[:, :], column, float(N - 1), None, ALU.min).then_inc(merge_asked, 1)
                dve.tensor_scalar(dst_diag[:, :], ident[:, :], column, None, ALU.mult).then_inc(diag_ready, 1)

            def merge_equal(column, number):
                dve.wait_ge(dst_spread, number)
                dve.tensor_scalar(equal[:, :], t_ps[1][:, 0:P], column, None, ALU.is_equal).then_inc(equal_ready, 1)
                dve.wait_ge(equal_ready, number)
                steps.up(dve.tensor_tensor_reduce(equal_earlier[:, :], equal[:, :], earlier[:, :], 1.0, 0.0,
                                                  ALU.mult, ALU.add, repeats[:, :]))
                steps.settle()
                steps.up(dve.tensor_scalar(first_of[:, :], repeats[:, :], 0.0, None, ALU.is_equal))
                steps.up(dve.tensor_scalar(shifted[:, :], column, float(NOWHERE), None, ALU.subtract))
                steps.settle()
                steps.up(dve.tensor_tensor(first_of[:, :], first_of[:, :], shifted[:, :], ALU.mult))
                steps.settle()
                steps.up(dve.tensor_scalar(merge_out[:, :], first_of[:, :], float(NOWHERE), None, ALU.add))

            def merge_finish(totals, number):
                dve.wait_ge(merged, number)
                dve.wait_ge(merge_gathered, number * 16)
                steps.settle()
                dve.tensor_tensor(new_rows[:, :], table_rows[:, :], totals, ALU.add).then_inc(merge_rows_ready, 1)

            dve.memset(dst_sb[96:P, LAST_COLS:EDGE_COLS], NOWHERE).then_inc(pads_set, 1)
            dve.memset(nxt_sb[96:P, LAST_COLS - 1:EDGE_COLS], NOWHERE).then_inc(pads_set, 1)
            dve.memset(src_sb[96:P, LAST_COLS:EDGE_COLS], 0).then_inc(pads_set, 1)
            dve.memset(msg[:, :, :], 1.0).then_inc(dve_set, 1)
            dve.memset(same_run[:, :, :], 0.0).then_inc(dve_set, 1)
            dve.memset(run_sum[:, :, :], 0.0).then_inc(dve_set, 1)
            dve.memset(first_sum[:, :], 0.0).then_inc(dve_set, 1)
            dve.memset(tile_msg[:, :], 1.0).then_inc(dve_set, 1)
            dve.memset(tile_x[:, 2 * D:4 * D], 0.0).then_inc(dve_set, 1)
            dve.memset(dst_of_slot[:, 0:1], -1.0).then_inc(dve_set, 1)
            dve.memset(dst_of_slot[:, SLOTS + 1:SLOTS + 2], float(NOWHERE)).then_inc(dve_set, 1)
            dve.wait_ge(edges_in, 16 * EDGE_LOADS)
            steps.up(dve.tensor_tensor(work_a[:, :], src_sb[:, :], dst_sb[:, :], ALU.is_equal))
            steps.up(dve.tensor_tensor(work_b[:, :], nxt_sb[:, :], dst_sb[:, :], ALU.not_equal))
            steps.settle()
            steps.up(dve.tensor_tensor_reduce(work_a[:, :], work_a[:, :], work_b[:, :], 1.0, 0.0,
                                              ALU.mult, ALU.add, stats[:, 0:1]))
            steps.settle()
            steps.up(dve.tensor_tensor_reduce(work_b[:, :], dst_sb[:, :], nxt_sb[:, :], 1.0, 0.0,
                                              ALU.subtract, ALU.max, largest_fall[:, :]))
            steps.up(dve.scalar_tensor_tensor(out=extra[:, :], in0=dst_sb[:, :], scalar=float(NOWHERE), in1=work_a[:, :],
                                              op0=ALU.is_lt, op1=ALU.subtract, accum_out=extras_in_row[:, :]))
            steps.settle()
            steps.up(dve.tensor_scalar(stats[:, 1:2], largest_fall[:, :], 0.0, None, ALU.is_gt))
            steps.up(dve.tensor_scalar(stats[:, 2:3], extras_in_row[:, :], float(SLOTS), None, ALU.is_gt))
            steps.settle()
            dve.drain().then_inc(stats_ready, 1)
            dve.wait_ge(consts_set, 4)
            steps.up(dve.tensor_tensor(key[:, :], extra[:, :], countdown[:, :], ALU.mult))
            steps.up(dve.tensor_tensor(nxt_sb[:, :], extra[:, :], src_sb[:, :], ALU.mult))
            steps.settle()
            steps.up(dve.tensor_scalar(key[:, :], key[:, :], SRC_BITS, None, ALU.logical_shift_left))
            steps.settle()
            steps.up(dve.tensor_tensor(key[:, :], key[:, :], nxt_sb[:, :], ALU.bitwise_or))
            dve.wait_ge(totals_ready, 1)
            dve.wait_ge(zeros_set, 5)
            steps.up(dve.tensor_scalar(checks[:, 0:1], extra_ps[:, 0:1], float(N), None, ALU.is_equal))
            steps.up(dve.tensor_scalar(checks[:, 1:3], extra_ps[:, 1:3], 0.0, None, ALU.is_equal))
            steps.up(dve.tensor_tensor(node_base[:, :], row_start[:, :], extra_ps[:, 4:5], ALU.subtract))
            steps.settle()
            steps.up(dve.tensor_tensor(flag_f[:, :], checks[:, 0:1], checks[:, 1:2], ALU.mult))
            steps.settle()
            steps.up(dve.tensor_tensor(flag_f[:, :], flag_f[:, :], checks[:, 2:3], ALU.mult))
            steps.up(dve.tensor_scalar(slot_base[:, :], minus_slot[:, :], node_base[:, 0:1], None, ALU.add))
            steps.settle()
            dve.tensor_copy(flag[:, :], flag_f[:, :]).then_inc(flag_ready, 1)
            dve.wait_ge(weights_in, 16 * (WEIGHT_LOADS - 1))
            dve.tensor_scalar(base_tile[:, :, :], base_row[:, :].unsqueeze(1).to_broadcast([P, NPP, ROW]),
                              flag_f[:, 0:1], None, ALU.mult).then_inc(base_ready, 1)
            dve.wait_ge(dve_set, 8)

            def search(pair, i):
                steps.settle()
                steps.up(dve.memset(mark[:, :], 0.0))
                steps.up(dve.max(out=top[:, :], in_=key_f))
                steps.settle()
                steps.up(dve.memset(mark[:, :], 0.0))
                steps.up(dve.match_replace(out=key_f, in_to_replace=top[:, :], in_values=key_f, imm_value=0.0))
                wait(dve, batch_gathered[i], pair * (16 * 2 * TOP))
                steps.up(dve.tensor_scalar(src_index[:, i, :], top_bits, (1 << SRC_BITS) - 1, None, ALU.bitwise_and))
                steps.up(dve.tensor_scalar(key_count[:, :], top_bits, SRC_BITS, None, ALU.logical_shift_right))
                steps.settle()
                steps.up(dve.tensor_scalar(found[:, :], key_count[:, :], 0.0, None, ALU.is_gt))
                steps.up(dve.tensor_tensor(slot_dst[:, :], slot_base[:, bass.ds(pair * (2 * TOP) + i * TOP, TOP)],
                                           key_count[:, :], ALU.subtract))
                steps.settle()
                steps.up(dve.tensor_tensor(dst_index[:, i, :], slot_dst[:, :], found[:, :], ALU.mult))
                steps.up(dve.scalar_tensor_tensor(out=slot_dst[:, :], in0=slot_dst[:, :], scalar=float(NOWHERE),
                                                  in1=found[:, :], op0=ALU.subtract, op1=ALU.mult))
                steps.settle()
                dve.tensor_scalar(dst_of_slot[:, bass.ds(pair * (2 * TOP) + i * TOP + 1, TOP)], slot_dst[:, :],
                                  float(NOWHERE), None, ALU.add).then_inc(slots_found, 1)

            def difference(pair, i):
                dve.wait_ge(batch_gathered[i], pair * (16 * 2 * TOP) + 16 * 2 * TOP)
                dve.tensor_tensor(gathered[:, i, :, D:2 * D], gathered[:, i, :, D:2 * D], gathered[:, i, :, 0:D],
                                  ALU.subtract).then_inc(difference_ready, 1)

            def runs(pair, i, last=False):
                here = dst_of_slot[:, bass.ds(pair * (2 * TOP) + i * TOP + 1, TOP)]
                left = dst_of_slot[:, bass.ds(pair * (2 * TOP) + i * TOP, TOP)]
                right = dst_of_slot[:, bass.ds(pair * (2 * TOP) + i * TOP + 2, TOP)]
                steps.settle()
                wait(dve, rows_ready, pair * 2 + i)
                steps.up(dve.tensor_copy(msg[:, :, 0:1], run_sum[:, :, TOP:TOP + 1]))
                dve.wait_ge(slots_found, BATCHES if last else pair * 2 + i + 2)
                steps.up(dve.tensor_tensor(same_run[:, :, 1:TOP + 1], here.unsqueeze(1).to_broadcast([P, ROW, TOP]),
                                           left.unsqueeze(1).to_broadcast([P, ROW, TOP]), ALU.is_equal))
                steps.up(dve.tensor_scalar(is_first[:, :], here, dst_of_slot[:, 1:2], None, ALU.is_equal))
                steps.up(dve.tensor_scalar(not_first[:, :], here, dst_of_slot[:, 1:2], None, ALU.not_equal))
                steps.up(dve.tensor_tensor(run_end[:, :], here, right, ALU.not_equal))
                dve.wait_ge(msg_done, pair * HALF_LEN + HALF_TURN.index("X") + 3 * i + 1)
                dve.tensor_tensor(msg[:, 0:D, 1:TOP + 1], extra_ps[:, 0:TOP * D].rearrange("p (s f) -> p f s", f=D),
                                  base_row[:, 0:D].unsqueeze(2).to_broadcast([P, D, TOP]), ALU.add).then_inc(extras_taken, 1)
                dve.wait_ge(extras_taken, pair * 2 + i + 1)
                steps.settle()
                steps.up(dve.tensor_tensor_scan(run_sum[:, :, :].rearrange("p f s -> p (f s)"),
                                                same_run[:, :, :].rearrange("p f s -> p (f s)"),
                                                msg[:, :, :].rearrange("p f s -> p (f s)"), 0.0, ALU.mult, ALU.add))
                steps.up(dve.tensor_tensor(first_part[:, :, :], msg[:, :, 1:TOP + 1],
                                           is_first[:, :].unsqueeze(1).to_broadcast([P, ROW, TOP]), ALU.mult))
                steps.up(dve.tensor_tensor(run_end[:, :], run_end[:, :], not_first[:, :], ALU.mult))
                steps.settle()
                steps.up(dve.tensor_reduce(first_add[:, :], first_part[:, :, :], AX.X, ALU.add))
                steps.up(dve.scalar_tensor_tensor(out=run_end[:, :], in0=here, scalar=float(NOWHERE), in1=run_end[:, :],
                                                  op0=ALU.subtract, op1=ALU.mult))
                wait(dve, rows_stored[i], pair * (16 * TOP))
                steps.up(dve.tensor_tensor(rows_out[:, i, :, :], run_sum[:, :, 1:TOP + 1].rearrange("p f s -> p s f"),
                                           base_row[:, :].unsqueeze(1).to_broadcast([P, TOP, ROW]), ALU.add))
                steps.settle()
                steps.up(dve.tensor_tensor(first_sum[:, :], first_sum[:, :], first_add[:, :], ALU.add))
                dve.tensor_scalar(out_index[:, i, :], run_end[:, :], float(NOWHERE), None, ALU.add).then_inc(rows_ready, 1)

            before_ways = steps.n
            way = take_way(dve)
            with dve.If(way == 1):
                search(0, 0)
                search(0, 1)
                difference(0, 0)
                search(1, 0)
                difference(0, 1)

                def two_batches(pair):
                    runs(pair, 0)
                    search(pair + 1, 1)
                    difference(pair + 1, 0)
                    runs(pair, 1)
                    search(pair + 2, 0)
                    difference(pair + 1, 1)

                two_batches(0)
                start, built = steps.n, steps.built
                with dve.Fori(1, BATCHES // 2 - 2) as pair:
                    steps.n = (pair - 1) * CHAIN_STEPS + start
                    two_batches(pair)
                assert steps.built == built + CHAIN_STEPS
                steps.n = start + (BATCHES // 2 - 3) * CHAIN_STEPS
                pair = BATCHES // 2 - 2
                runs(pair, 0)
                search(pair + 1, 1)
                difference(pair + 1, 0)
                runs(pair, 1)
                difference(pair + 1, 1)
                runs(pair + 1, 0)
                runs(pair + 1, 1, last=True)
                steps.settle()
                merge_start(dst_of_slot[:, 1:2], 1)
                merge_equal(dst_of_slot[:, 1:2], 1)
                merge_finish(extra_ps[:, 256:256 + ROW], 1)
            with dve.If(way == 0):
                dve.wait_ge(base_ready, 1)
                steps.n = before_ways
                def dve_tile(t):
                    steps.settle()
                    wait(dve, merge_stored, t * 16)
                    steps.up(dve.tensor_copy(merge_dst[:, :], dst_sb[:, bass.ds(t, 1)]))
                    steps.up(dve.tensor_copy(merge_src[:, :], src_sb[:, bass.ds(t, 1)]))
                    steps.settle()
                    merge_start(merge_dst[:, 0:1], t + 1)
                    dve.wait_ge(tile_gathered, t * 32 + 32)
                    dve.tensor_tensor(tile_x[:, D:2 * D], tile_x[:, D:2 * D], tile_x[:, 0:D], ALU.subtract).then_inc(tile_diff, 1)
                    merge_equal(merge_dst[:, 0:1], t + 1)
                    dve.wait_ge(tile_pe, t * 7 + 7)
                    dve.tensor_tensor(tile_msg[:, 0:D], extra_ps[:, 0:D], base_row[:, 0:D], ALU.add).then_inc(tile_msg_ready, 1)
                    merge_finish(self_ps[:, 0:ROW], t + 1)

                dve_tile(0)
                start, built = steps.n, steps.built
                with dve.Fori(1, EDGE_COLS) as t:
                    steps.n = (t - 1) * MERGE_STEPS + start
                    dve_tile(t)
                assert steps.built == built + MERGE_STEPS

            def dve_last(b, i, round_):
                dve.wait_ge(last_loaded[i], round_ * 32 + 32)
                last_steps.up(dve.tensor_scalar(counts[:, i, :], sums[:, i, :, D], 1.0, None, ALU.max))
                last_steps.settle()
                dve.reciprocal(share[:, i, :], counts[:, i, :]).then_inc(share_ready, 1)
                dve.wait_ge(mean_ready, b + 1)
                dve.tensor_tensor(y, x_last[:, i, :, :], mean_msg[:, i, :, :], ALU.add).then_inc(y_ready, 1)
                dve.wait_ge(y_ready, b + 1)
                last_steps.up(dve.tensor_reduce(y_sum[:, :], y, AX.X, ALU.add))
                last_steps.settle()
                last_steps.up(dve.tensor_scalar(y_mean[:, :], y_sum[:, :], 1.0 / D, None, ALU.mult))
                last_steps.settle()
                wait(dve, result_stored[i], round_ * 16)
                dve.tensor_tensor(centred[:, i, :, :], y, y_mean[:, :].unsqueeze(2).to_broadcast([P, NPP, D]),
                                  ALU.subtract).then_inc(centred_ready, 1)

            def dve_scale(b, i):
                dve.wait_ge(square_ready, b + 1)
                last_steps.up(dve.tensor_reduce(y_var[:, :], square[:, i, :, :], AX.X, ALU.add))
                last_steps.settle()
                dve.tensor_scalar(var[:, i, :], y_var[:, :], 1.0 / D, EPS, ALU.mult, ALU.add).then_inc(var_ready, 1)
                dve.wait_ge(std_ready, b + 1)
                last_steps.up(dve.reciprocal(rstd[:, :], std[:, i, :]))
                last_steps.settle()
                dve.tensor_tensor(result[:, i, :, :], centred[:, i, :, :],
                                  rstd[:, :].unsqueeze(2).to_broadcast([P, NPP, D]), ALU.mult).then_inc(result_ready, 1)

            dve_last(0, 0, 0)
            dve_last(1, 1, 0)
            dve_scale(0, 0)
            start, built = last_steps.n, last_steps.built
            with dve.Fori(1, FULL // 2) as pair:
                last_steps.n = (pair - 1) * LAST_STEPS + start
                dve_last(pair * 2, 0, pair)
                dve_scale(pair * 2 - 1, 1)
                dve_last(pair * 2 + 1, 1, pair)
                dve_scale(pair * 2, 0)
            assert last_steps.built == built + LAST_STEPS
            last_steps.n = start + (FULL // 2 - 1) * LAST_STEPS
            dve_last(FULL, 0, FULL // 2)
            dve_scale(FULL - 1, 1)
            dve_scale(FULL, 0)


_INS = ["x", "src", "dst", "L0_gnn_W1", "L0_gnn_b1", "L0_gnn_W2", "L0_gnn_b2", "L0_gnn_W3", "L0_gnn_b3",
        "L0_gnn_W4", "L0_gnn_b4"]


def kernel(**inputs):
    import numpy as np
    import concourse.bacc as bacc
    from concourse.bass_utils import run_bass_kernel_spmd

    nc = bacc.Bacc("TRN2", target_bir_lowering=False, num_devices=1)
    arrays, args = {}, []
    for name in _INS:
        a = np.ascontiguousarray(inputs[name])
        arrays[f"in_{name}"] = a
        args.append(nc.dram_tensor(f"in_{name}", a.shape, mybir.dt.from_np(a.dtype), kind="ExternalInput").ap())
    out = nc.dram_tensor("out_0", arrays["in_x"].shape, F32, kind="ExternalOutput").ap()
    gnn_program(nc, *args, out)
    r = run_bass_kernel_spmd(nc, [arrays], core_ids=[0])
    return r.results[0]["out_0"]
```

```python
import concourse.bass as bass
from concourse import mybir
from contextlib import ExitStack

F32 = mybir.dt.float32
I32 = mybir.dt.int32
ALU = mybir.AluOpType
ACT = mybir.ActivationFunctionType
AX = mybir.AxisListType

P = 128
EPS = 1e-5
NOWHERE = 1 << 20
SRC_BITS = 17
TOP = 8


def wait(eng, sem, value):
    if isinstance(value, int) and value <= 0:
        return
    eng.wait_ge(sem, value)


class Count:

    def __init__(self, eng, sem):
        self.eng, self.sem, self.n = eng, sem, 0
        self.built = 0

    def up(self, instruction):
        instruction.then_inc(self.sem, 1)
        self.n = self.n + 1
        self.built += 1

    def settle(self):
        wait(self.eng, self.sem, self.n)


def gnn_program(nc, x, src, dst, W1, b1, W2, b2, W3, b3, W4, b4, out):
    N, D = x.shape
    E = src.shape[0]
    H1, H2, H3 = W1.shape[1], W2.shape[1], W3.shape[1]
    ROW = D + 1
    assert (2 * D, H1, H2, H3, W4.shape[1]) == (64, 64, 128, 64, 32) and N < 1 << SRC_BITS

    EDGE_COLS = -(-E // P)
    LAST_COLS = E - (P - 1) * EDGE_COLS
    SLOTS = 240
    BATCHES = SLOTS // TOP
    CHAIN_STEPS = 4 * (10 + 12) + 6 * 2
    MERGE_STEPS = 2 + 5
    LAST_STEPS = 4 * 2
    LAST_RING = 4
    TABLE_PARTS = 6
    TURN_MARKS, TILE_MARKS = 4 * 3, 4
    KEY_TOP = 2048 + EDGE_COLS

    NPP = 16
    BLOCK = P * NPP
    FULL = N // BLOCK
    REST = (N - FULL * BLOCK) // NPP
    BLOCKS = FULL + 1
    assert 0 < REST < P and (N - FULL * BLOCK) % NPP == 0 and FULL % LAST_RING == 0

    HALF_TURN = "ABABXABX"
    HALF_LEN, HALF_BLOCKS, HALF_TILES = len(HALF_TURN), 3, 5
    PATTERN = HALF_TURN * 2
    LEN = len(PATTERN)
    TURNS = BATCHES // 4
    UNITS = PATTERN * TURNS + HALF_TURN + "AB" * (BLOCKS - HALF_BLOCKS * (2 * TURNS + 1))
    assert BATCHES == 4 * TURNS + 2 and UNITS.count("A") == BLOCKS and UNITS.count("X") == BATCHES
    RING = HALF_BLOCKS
    TILE_OF = [sum(k != "B" for k in UNITS[:u + 1]) - 1 for u in range(len(UNITS))]
    NUMBER_OF = [UNITS[:u + 1].count("X" if UNITS[u] == "X" else "A") - 1 for u in range(len(UNITS))]
    TILE_OF_BLOCK = [TILE_OF[u] for u in range(len(UNITS)) if UNITS[u] == "A"]
    FREE_AT = [max([v + 1 for v in range(len(UNITS)) if TILE_OF[v] == TILE_OF[u] - 2], default=0)
               for u in range(len(UNITS))]
    PER_TURN = {"unit": LEN, "tile": 2 * HALF_TILES, "A": 2 * HALF_BLOCKS, "X": 4}

    def exists(turn, pos):
        return not isinstance(turn, int) or 0 <= turn * LEN + pos < len(UNITS)

    def kind(turn, pos):
        return UNITS[turn * LEN + pos] if isinstance(turn, int) else UNITS[LEN + pos]

    def at(turn, pos, numbers, step):
        if isinstance(turn, int):
            return numbers[turn * LEN + pos]
        return (turn - 1) * step + numbers[LEN + pos]

    def tile_of(turn, pos):
        return at(turn, pos, TILE_OF, PER_TURN["tile"])

    def number_of(turn, pos):
        return at(turn, pos, NUMBER_OF, PER_TURN["X" if kind(turn, pos) == "X" else "A"])

    def place_of(turn, pos, numbers, ring):
        return numbers[turn * LEN + pos if isinstance(turn, int) else LEN + pos] % ring

    def run_steps(eng, step, prologue):
        prologue()
        for pos in range(LEN):
            step(0, pos)
        with eng.Fori(1, TURNS) as turn:
            for pos in range(LEN):
                step(turn, pos)
        for pos in range(len(UNITS) - TURNS * LEN + 3):
            step(TURNS, pos)

    table = nc.dram_tensor("sums_of_messages", (N, ROW), F32).ap()
    x_centred = nc.dram_tensor("x_less_its_mean", (N, D), F32).ap()
    xc_blocks = x_centred[0:FULL * BLOCK, :].rearrange("(b p c) f -> b p (c f)", p=P, c=NPP)
    xc_rest = x_centred[FULL * BLOCK:N, :].rearrange("(p c) f -> p (c f)", c=NPP)
    x_blocks = x[0:FULL * BLOCK, :].rearrange("(b p c) f -> b p (c f)", p=P, c=NPP)
    x_rest = x[FULL * BLOCK:N, :].rearrange("(p c) f -> p (c f)", c=NPP)
    out_blocks = out[0:FULL * BLOCK, :].rearrange("(b p c) f -> b p (c f)", p=P, c=NPP)
    out_rest = out[FULL * BLOCK:N, :].rearrange("(p c) f -> p (c f)", c=NPP)
    table_blocks = table[0:FULL * BLOCK, :].rearrange("(b p c) f -> b p (c f)", p=P, c=NPP)
    table_rest = table[FULL * BLOCK:N, :].rearrange("(p c) f -> p (c f)", c=NPP)

    with ExitStack() as ctx:
        def sb(name, shape, dt=F32):
            return ctx.enter_context(nc.sbuf_tensor(name, shape, dt))

        def sem(name):
            return ctx.enter_context(nc.semaphore(name))

        src_sb = sb("src_sb", [P, EDGE_COLS], I32)
        dst_sb = sb("dst_sb", [P, EDGE_COLS], I32)
        nxt_sb = sb("nxt_sb", [P, EDGE_COLS], I32)
        key = sb("key", [P, EDGE_COLS], I32)
        key_f = key[:, :].bitcast(F32)
        work_a = sb("work_a", [P, EDGE_COLS])
        work_b = sb("work_b", [P, EDGE_COLS])
        extra = sb("extra", [P, EDGE_COLS])
        countdown = sb("countdown", [P, EDGE_COLS], I32)
        self_msg = sb("self_msg", [P, BLOCKS, NPP * D])

        ident = sb("ident", [P, P])
        ones = sb("ones", [P, P])
        before = sb("before", [P, P])
        earlier = sb("earlier", [P, P])
        w1_pair = sb("w1_pair", [P, P])
        w1_self = sb("w1_self", [P, P])
        w2_twice = sb("w2_twice", [P, P])
        w3_sb = sb("w3_sb", [P, H3])
        w4_pair = sb("w4_pair", [P, 2 * D])
        w4_sum = sb("w4_sum", [P, 2])
        w4_mean = sb("w4_mean", [P, 2])
        b1_sb = sb("b1_sb", [P, 1])
        b2_sb = sb("b2_sb", [P, 1])
        b3_sb = sb("b3_sb", [P, 1])
        base_row = sb("base_row", [P, ROW])
        base_tile = sb("base_tile", [P, NPP, ROW])

        stats = sb("stats", [P, 3])
        largest_fall = sb("largest_fall", [P, 1])
        extras_in_row = sb("extras_in_row", [P, 1])
        checks = sb("checks", [P, 3])
        flag_f = sb("flag_f", [P, 1])
        flag = sb("flag", [P, 1], I32)
        row_start = sb("row_start", [P, 1])
        node_base = sb("node_base", [P, 1])
        minus_slot = sb("minus_slot", [P, SLOTS])
        slot_base = sb("slot_base", [P, SLOTS])

        top = sb("top", [P, TOP])
        top_bits = top[:, :].bitcast(I32)
        mark = sb("mark", [P, 1])
        pool_mark = sb("pool_mark", [P, 1])
        key_count = sb("key_count", [P, TOP], I32)
        found = sb("found", [P, TOP])
        slot_dst = sb("slot_dst", [P, TOP])
        dst_of_slot = sb("dst_of_slot", [P, SLOTS + 2])
        src_index = sb("src_index", [P, 4, TOP], I32)
        dst_index = sb("dst_index", [P, 4, TOP], I32)
        out_index = sb("out_index", [P, 4, TOP], I32)
        gathered = sb("gathered", [P, 4, TOP, 2 * D])
        x_in = sb("x_in", [P, RING, NPP * D])
        x_mid = sb("x_mid", [P, RING, NPP * D])
        x_sum = sb("x_sum", [P, NPP])
        x_mean = sb("x_mean", [P, NPP])
        xT = sb("xT", [P, 2, 512])
        h1 = sb("h1", [P, 2, 512])
        h2 = sb("h2", [P, 2, 2, 512])
        h3 = sb("h3", [P, 2, 512])
        msg = sb("msg", [P, ROW, TOP + 1])
        same_run = sb("same_run", [P, ROW, TOP + 1])
        run_sum = sb("run_sum", [P, ROW, TOP + 1])
        first_part = sb("first_part", [P, ROW, TOP])
        first_add = sb("first_add", [P, ROW])
        first_sum = sb("first_sum", [P, ROW])
        is_first = sb("is_first", [P, TOP])
        run_end = sb("run_end", [P, TOP])
        not_first = sb("not_first", [P, TOP])
        rows_out = sb("rows_out", [P, 4, TOP, ROW])

        merge_dst = sb("merge_dst", [P, 1])
        merge_index = sb("merge_index", [P, 1], I32)
        merge_out = sb("merge_out", [P, 1], I32)
        merge_src = sb("merge_src", [P, 1], I32)
        dst_diag = sb("dst_diag", [P, P])
        equal = sb("equal", [P, P])
        equal_earlier = sb("equal_earlier", [P, P])
        repeats = sb("repeats", [P, 1])
        shifted = sb("shifted", [P, 1])
        first_of = sb("first_of", [P, 1])
        table_rows = sb("table_rows", [P, ROW])
        new_rows = sb("new_rows", [P, ROW])
        tile_msg = sb("tile_msg", [P, ROW])
        tile_x = sb("tile_x", [P, 4 * D])

        x_last = sb("x_last", [P, LAST_RING, NPP, D])
        sums = sb("sums", [P, LAST_RING, NPP, ROW])
        y = h2[:, :, :, :].rearrange("p a b n -> p (a b n)").rearrange("p (i c f) -> p i c f", i=LAST_RING, f=D)
        result = gathered[:, :, :, :].rearrange("p i s f -> p (i s f)").rearrange("p (i c f) -> p i c f", i=LAST_RING, f=D)
        square = xT[:, :, :].rearrange("p i (c f) -> p i c f", f=D)

        def small(tile, place):
            return tile[:, place * LAST_RING * NPP:(place + 1) * LAST_RING * NPP].rearrange("p (i c) -> p i c", c=NPP)

        counts, share, square_sum, std = small(work_a, 0), small(work_a, 1), small(work_a, 2), small(work_a, 3)
        rstd = work_a[:, 4 * LAST_RING * NPP:4 * LAST_RING * NPP + NPP]
        eps = sb("eps", [P, 1])

        def bank(name):
            return ctx.enter_context(nc.psum_tensor(name, [P, 512], F32))

        t_ps = [bank("t_ps0"), bank("t_ps1")]
        h1_ps, h2a_ps, h2b_ps, h3_ps = bank("h1_ps"), bank("h2a_ps"), bank("h2b_ps"), bank("h3_ps")
        self_ps, extra_ps = bank("self_ps"), bank("extra_ps")
        h2_ps = [h2a_ps, h2b_ps]

        pads_set = sem("pads_set")
        edges_in = sem("edges_in")
        zeros_set = sem("zeros_set")
        dve_set = sem("dve_set")
        weights_in = sem("weights_in")
        consts_set = sem("consts_set")
        pool_steps = sem("pool_steps")
        pool_marks = sem("pool_marks")
        dve_steps = sem("dve_steps")
        dve_last_steps = sem("dve_last_steps")
        stats_ready = sem("stats_ready")
        totals_ready = sem("totals_ready")
        flag_ready = sem("flag_ready")
        table_started = sem("table_started")
        base_ready = sem("base_ready")
        w4_ready = sem("w4_ready")

        x_loaded = [sem(f"x_loaded{i}") for i in range(RING)]
        slots_found = sem("slots_found")
        batch_gathered = [sem(f"batch_gathered{i}") for i in range(4)]
        difference_ready = sem("difference_ready")
        transposed = sem("transposed")
        xT_ready = sem("xT_ready")
        h1_done, h1_ready = sem("h1_done"), sem("h1_ready")
        h2_done, h2_ready = sem("h2_done"), sem("h2_ready")
        h3_done, h3_ready = sem("h3_done"), sem("h3_ready")
        msg_done = sem("msg_done")
        self_stored = sem("self_stored")
        extras_taken = sem("extras_taken")
        rows_ready = sem("rows_ready")
        rows_stored = [sem(f"rows_stored{i}") for i in range(4)]

        merge_asked = sem("merge_asked")
        diag_ready = sem("diag_ready")
        dst_spread = sem("dst_spread")
        equal_ready = sem("equal_ready")
        merged = sem("merged")
        merge_gathered = sem("merge_gathered")
        merge_rows_ready = sem("merge_rows_ready")
        merge_stored = sem("merge_stored")
        tile_gathered = sem("tile_gathered")
        tile_diff = sem("tile_diff")
        tile_pe = sem("tile_pe")
        tile_act = sem("tile_act")
        tile_msg_ready = sem("tile_msg_ready")

        table_done = sem("table_done")
        self_done = sem("self_done")
        last_loaded = [sem(f"last_loaded{i}") for i in range(LAST_RING)]
        share_ready = sem("share_ready")
        mean_added = sem("mean_added")
        mean_ready = sem("mean_ready")
        y_ready = sem("y_ready")
        square_ready = sem("square_ready")
        square_summed = sem("square_summed")
        std_ready = sem("std_ready")
        result_ready = sem("result_ready")
        result_stored = [sem(f"result_stored{i}") for i in range(LAST_RING)]
        centred_made = sem("centred_made")
        centred_stored = [sem(f"centred_stored{i}") for i in range(RING)]

        WEIGHT_LOADS = 18
        EDGE_LOADS = 9
        SPLIT = (P - 1) // 16 * 16

        def take_way(eng):
            eng.wait_ge(flag_ready, 1)
            return eng.value_load(flag[0:1, 0:1], min_val=0, max_val=1)

        block = ctx.enter_context(nc.Block())

        @block.sync
        def _(sp):
            sp.wait_ge(pads_set, 3)
            for tile, flat, n in ((dst_sb, dst, E), (nxt_sb, dst[1:E], E - 1), (src_sb, src, E)):
                for lo, hi in ((0, SPLIT), (SPLIT, P - 1)):
                    sp.dma_start(tile[lo:hi, :], flat[lo * EDGE_COLS:hi * EDGE_COLS].rearrange(
                        "(p c) -> p c", c=EDGE_COLS)).then_inc(edges_in, 16)
                cols = n - (P - 1) * EDGE_COLS
                sp.dma_start(tile[P - 1:P, 0:cols], flat[(P - 1) * EDGE_COLS:n].rearrange(
                    "(p c) -> p c", p=1)).then_inc(edges_in, 16)

            def load_block(b, ring, tiles, rest=False):
                wait(sp, transposed, tiles)
                if rest:
                    sp.dma_start(x_in[0:REST, ring, :], x_rest).then_inc(x_loaded[ring], 16)
                else:
                    sp.dma_start(x_in[:, ring, :], x_blocks[b]).then_inc(x_loaded[ring], 16)

            def store_block(b, ring):
                wait(sp, centred_made, b + 1)
                sp.dma_start(xc_blocks[b], x_mid[:, ring, :]).then_inc(centred_stored[ring], 16)

            def start_table(part):
                n = FULL // TABLE_PARTS
                sp.dma_start(table_blocks[part * n:(part + 1) * n].rearrange("b p n -> p b n"),
                             base_tile[:, :, :].rearrange("p c f -> p (c f)").unsqueeze(1).to_broadcast([P, n, NPP * ROW])
                             ).then_inc(table_started, 16)

            def rest_of_blocks(tiles):
                store_block(FULL - RING, FULL % RING)
                load_block(FULL, FULL % RING, tiles, rest=True)
                for b in range(FULL - RING + 1, FULL):
                    store_block(b, b % RING)
                wait(sp, centred_made, BLOCKS)
                sp.dma_start(xc_rest, x_mid[0:REST, FULL % RING, :]).then_inc(centred_stored[FULL % RING], 16)

            for b in range(RING):
                load_block(b, b, 0)
            way = take_way(sp)
            sp.wait_ge(base_ready, 1)
            sp.dma_start(table_rest, base_tile[0:REST, :, :].rearrange("p c f -> p (c f)")).then_inc(table_started, 16)
            with sp.If(way == 1):
                for b in range(RING, RING + TABLE_PARTS):
                    start_table(b - RING)
                    store_block(b - RING, b % RING)
                    load_block(b, b % RING, TILE_OF_BLOCK[b - RING] + 1)
                with sp.Fori(1 + TABLE_PARTS // RING, FULL // RING) as half:
                    for r in range(RING):
                        store_block((half - 1) * RING + r, r)
                        load_block(half * RING + r, r, (half - 1) * HALF_TILES + TILE_OF_BLOCK[r] + 1)
                rest_of_blocks(TILE_OF_BLOCK[FULL - RING] + 1)
            with sp.If(way == 0):
                for part in range(TABLE_PARTS):
                    start_table(part)
                with sp.Fori(1, FULL // RING) as half:
                    for r in range(RING):
                        store_block((half - 1) * RING + r, r)
                        load_block(half * RING + r, r, 0)
                rest_of_blocks(0)

            for ring in range(RING):
                sp.wait_ge(centred_stored[ring], 16 * len(range(ring, BLOCKS, RING)))
            sp.wait_ge(table_done, 1)

            def load_last(b, i, rest=False):
                wait(sp, y_ready, b - LAST_RING + 1)
                if rest:
                    sp.dma_start(sums[0:REST, i, :, :], table_rest).then_inc(last_loaded[i], 16)
                    sp.dma_start(x_last[0:REST, i, :, :], xc_rest).then_inc(last_loaded[i], 16)
                else:
                    sp.dma_start(sums[:, i, :, :], table_blocks[b]).then_inc(last_loaded[i], 16)
                    sp.dma_start(x_last[:, i, :, :], xc_blocks[b]).then_inc(last_loaded[i], 16)

            for i in range(LAST_RING):
                load_last(i, i)
            with sp.Fori(1, FULL // LAST_RING) as turn:
                for i in range(LAST_RING):
                    load_last(turn * LAST_RING + i, i)
            load_last(FULL, 0, rest=True)

        @block.scalar
        def _(act):
            act.wait_ge(zeros_set, 5)
            act.wait_ge(dve_set, 9)

            def column(v):
                return v.rearrange("(n a) -> n a", a=1)

            loads = []
            for h in (0, 1):
                loads += [(w1_pair[64 * h:64 * h + 64, 64 * h:64 * h + 64], W1),
                          (w2_twice[64 * h:64 * h + 64, :], W2),
                          (w4_pair[64 * h:64 * h + 64, D * h:D * h + D], W4),
                          (b1_sb[64 * h:64 * h + 64, :], column(b1)),
                          (b3_sb[64 * h:64 * h + 64, :], column(b3))]
            for q in range(4):
                loads.append((w1_self[D * q:D * q + D, 64 * (q % 2):64 * (q % 2) + 64], W1[0:D, :]))
            loads += [(w3_sb[:, :], W3), (b2_sb[:, :], column(b2)),
                      (base_row[:, 0:D], b4.rearrange("(a n) -> a n", a=1).to_broadcast([P, D]))]
            assert len(loads) == WEIGHT_LOADS - 1
            for place, what in loads:
                act.dma_start(place, what).then_inc(weights_in, 16)

            way = take_way(act)
            with act.If(way == 1):
                act.wait_ge(weights_in, 16 * (WEIGHT_LOADS - 1))

                def act_step(turn, pos):
                    u = turn * LEN + pos
                    if exists(turn, pos + 1) and kind(turn, pos + 1) != "B":
                        par = place_of(turn, pos + 1, TILE_OF, 2)
                        act.wait_ge(transposed, tile_of(turn, pos + 1) + 1)
                        wait(act, h1_done, at(turn, pos + 1, FREE_AT, LEN))
                        act.activation(xT[:, par, :], t_ps[par][:, :], ACT.Copy).then_inc(xT_ready, 1)
                    if exists(turn, pos):
                        act.wait_ge(h1_done, u + 1)
                        wait(act, h2_done, (u - 1) * 2)
                        act.activation(h1[:, pos % 2, :], h1_ps[:, :], ACT.Relu, bias=b1_sb[:, 0:1]).then_inc(h1_ready, 1)
                    if exists(turn, pos - 1):
                        for j in range(2):
                            act.wait_ge(h2_done, (u - 1) * 2 + j + 1)
                            wait(act, h3_done, (u - 2) * 2)
                            act.activation(h2[:, (pos - 1) % 2, j, :], h2_ps[j][:, :], ACT.Relu,
                                           bias=b2_sb[:, 0:1]).then_inc(h2_ready, 1)
                    if exists(turn, pos - 2):
                        act.wait_ge(h3_done, (u - 1) * 2)
                        wait(act, msg_done, u - 3)
                        act.activation(h3[:, (pos - 2) % 2, :], h3_ps[:, :], ACT.Relu, bias=b3_sb[:, 0:1]).then_inc(h3_ready, 1)
                    if exists(turn, pos - 3) and kind(turn, pos - 3) != "X":
                        half = "AB".index(kind(turn, pos - 3))
                        act.wait_ge(msg_done, u - 2)
                        place = self_msg[:, bass.ds(number_of(turn, pos - 3), 1), :].rearrange(
                            "p b (k h n) -> p (b k) h n", k=4, h=2)
                        act.activation(place[:, :, half, :], self_ps[:, 0:256].rearrange("p (k n) -> p k n", k=4),
                                       ACT.Copy).then_inc(self_stored, 1)

                def first_tile():
                    act.wait_ge(transposed, 1)
                    act.activation(xT[:, 0, :], t_ps[0][:, :], ACT.Copy).then_inc(xT_ready, 1)

                run_steps(act, act_step, first_tile)
                act.drain().then_inc(self_done, 1)
            with act.If(way == 0):
                act.wait_ge(weights_in, 16 * (WEIGHT_LOADS - 1))
                def act_tile(t):
                    act.wait_ge(tile_pe, t * 7 + 1)
                    act.activation(xT[:, 0, 0:P], t_ps[0][:, 0:P], ACT.Copy).then_inc(tile_act, 1)
                    act.wait_ge(tile_pe, t * 7 + 2)
                    act.activation(h1[:, 0, 0:P], h1_ps[:, 0:P], ACT.Relu, bias=b1_sb[:, 0:1]).then_inc(tile_act, 1)
                    for j in range(2):
                        act.wait_ge(tile_pe, t * 7 + 3 + j)
                        act.activation(h2[:, 0, j, 0:P], h2_ps[j][:, 0:P], ACT.Relu, bias=b2_sb[:, 0:1]).then_inc(tile_act, 1)
                    act.wait_ge(tile_pe, t * 7 + 6)
                    act.activation(h3[:, 0, 0:P], h3_ps[:, 0:P], ACT.Relu, bias=b3_sb[:, 0:1]).then_inc(tile_act, 1)

                act_tile(0)
                with act.Fori(1, EDGE_COLS) as t:
                    act_tile(t)

            def act_last(b, i):
                if not isinstance(b, int) or b < BLOCKS:
                    act.wait_ge(y_ready, b + 1)
                    wait(act, square_summed, b - 1)
                    act.activation(square[:, i % 2, :, :], y[:, i, :, :], ACT.Square).then_inc(square_ready, 1)
                if not isinstance(b, int) or 1 <= b <= BLOCKS:
                    j = (i - 1) % LAST_RING
                    act.wait_ge(square_summed, b)
                    wait(act, result_ready, b - LAST_RING)
                    act.activation(std[:, j, :], square_sum[:, j, :], ACT.Sqrt, bias=eps[:, 0:1],
                                   scale=1.0 / D).then_inc(std_ready, 1)
                if not isinstance(b, int) or 2 <= b:
                    j = (i - 2) % LAST_RING
                    act.wait_ge(result_ready, b - 1)
                    if isinstance(b, int) and b - 2 == FULL:
                        act.dma_start(out_rest, result[0:REST, j, :, :]).then_inc(result_stored[j], 16)
                    else:
                        act.dma_start(out_blocks[b - 2], result[:, j, :, :]).then_inc(result_stored[j], 16)

            for b in range(LAST_RING):
                act_last(b, b)
            with act.Fori(1, FULL // LAST_RING) as turn:
                for i in range(LAST_RING):
                    act_last(turn * LAST_RING + i, i)
            for b in range(FULL, BLOCKS + 2):
                act_last(b, b % LAST_RING)
            for i in range(LAST_RING):
                act.wait_ge(result_stored[i], 16 * len(range(i, BLOCKS, LAST_RING)))

        @block.tensor
        def _(pe):
            pe.wait_ge(consts_set, 4)
            pe.wait_ge(stats_ready, 1)
            pe.matmul(extra_ps[:, 0:3], ones[:, :], stats[:, :], start=True, stop=True)
            pe.matmul(extra_ps[:, 4:5], before[:, :], extras_in_row[:, :], start=True, stop=True).then_inc(totals_ready, 1)

            def merge(number):
                pe.wait_ge(diag_ready, number)
                pe.matmul(t_ps[1][:, 0:P], ones[:, :], dst_diag[:, :], start=True, stop=True).then_inc(dst_spread, 1)
                pe.wait_ge(equal_ready, number)

            way = take_way(pe)
            with pe.If(way == 1):
                pe.wait_ge(weights_in, 16 * (WEIGHT_LOADS - 1))
                pe.wait_ge(w4_ready, 2)

                def transposes(turn, pos):
                    par = place_of(turn, pos, TILE_OF, 2)
                    wait(pe, xT_ready, tile_of(turn, pos) - 1)
                    if kind(turn, pos) == "X":
                        buf = place_of(turn, pos, NUMBER_OF, 4)
                        pe.wait_ge(difference_ready, number_of(turn, pos) + 1)
                        tile = gathered[:, buf, :, :].rearrange("p s f -> p (s f)")
                    else:
                        ring = place_of(turn, pos, NUMBER_OF, RING)
                        rounds = at(turn, pos, [n // RING for n in NUMBER_OF], 2)
                        pe.wait_ge(x_loaded[ring], rounds * 16 + 16)
                        tile = x_in[:, ring, :]
                    for j in range(4):
                        last = pe.transpose(t_ps[par][:, j * P:(j + 1) * P], tile[:, j * P:(j + 1) * P], ident[:, :])
                    last.then_inc(transposed, 1)

                def pe_step(turn, pos):
                    u = turn * LEN + pos
                    if exists(turn, pos + 1) and kind(turn, pos + 1) != "B":
                        transposes(turn, pos + 1)
                    if exists(turn, pos):
                        k, par = kind(turn, pos), place_of(turn, pos, TILE_OF, 2)
                        pe.wait_ge(xT_ready, tile_of(turn, pos) + 1)
                        wait(pe, h1_ready, u)
                        lo, hi = {"A": (0, 64), "B": (64, P), "X": (0, P)}[k]
                        w = w1_pair if k == "X" else w1_self
                        pe.matmul(h1_ps[:, :], w[lo:hi, :], xT[lo:hi, par, :], start=True, stop=True).then_inc(h1_done, 1)
                    if exists(turn, pos - 1):
                        pe.wait_ge(h1_ready, u)
                        for j in range(2):
                            wait(pe, h2_ready, (u - 2) * 2 + j + 1)
                            pe.matmul(h2_ps[j][:, :], w2_twice[64 * j:64 * j + 64, :],
                                      h1[64 * j:64 * j + 64, (pos - 1) % 2, :], start=True, stop=True).then_inc(h2_done, 1)
                    if exists(turn, pos - 2):
                        wait(pe, h3_ready, u - 2)
                        for j in range(2):
                            pe.wait_ge(h2_ready, (u - 2) * 2 + j + 1)
                            pe.matmul(h3_ps[64 * j:64 * j + 64, :], w3_sb[:, :], h2[:, (pos - 2) % 2, j, :],
                                      start=True, stop=True).then_inc(h3_done, 1)
                    if exists(turn, pos - 3):
                        k, number = kind(turn, pos - 3), number_of(turn, pos - 3)
                        pe.wait_ge(h3_ready, u - 2)
                        if k == "X":
                            wait(pe, extras_taken, number)
                        else:
                            wait(pe, self_stored, number * 2 + "AB".index(k))
                        place = extra_ps if k == "X" else self_ps
                        for j in range(4):
                            last = pe.matmul(place[:, 64 * j:64 * j + 64], h3[:, (pos - 3) % 2, j * P:(j + 1) * P],
                                             w4_pair[:, :], start=True, stop=True)
                        last.then_inc(msg_done, 1)

                run_steps(pe, pe_step, lambda: transposes(0, 0))
                merge(1)
                pe.matmul(extra_ps[:, 256:256 + ROW], equal[:, :], first_sum[:, :], start=True, stop=True).then_inc(merged, 1)

            with pe.If(way == 0):
                pe.wait_ge(weights_in, 16 * (WEIGHT_LOADS - 1))
                pe.wait_ge(w4_ready, 2)
                def pe_tile(t):
                    pe.wait_ge(tile_diff, t + 1)
                    pe.transpose(t_ps[0][:, 0:P], tile_x[:, :], ident[:, :]).then_inc(tile_pe, 1)
                    pe.wait_ge(tile_act, t * 5 + 1)
                    pe.matmul(h1_ps[:, 0:P], w1_pair[:, :], xT[:, 0, 0:P], start=True, stop=True).then_inc(tile_pe, 1)
                    pe.wait_ge(tile_act, t * 5 + 2)
                    for j in range(2):
                        pe.matmul(h2_ps[j][:, 0:P], w2_twice[64 * j:64 * j + 64, :], h1[64 * j:64 * j + 64, 0, 0:P],
                                  start=True, stop=True).then_inc(tile_pe, 1)
                    for j in range(2):
                        pe.wait_ge(tile_act, t * 5 + 3 + j)
                        pe.matmul(h3_ps[64 * j:64 * j + 64, 0:P], w3_sb[:, :], h2[:, 0, j, 0:P],
                                  start=True, stop=True).then_inc(tile_pe, 1)
                    pe.wait_ge(tile_act, t * 5 + 5)
                    pe.matmul(extra_ps[:, 0:64], h3[:, 0, 0:P], w4_pair[:, :], start=True, stop=True).then_inc(tile_pe, 1)
                    merge(t + 1)
                    pe.wait_ge(tile_msg_ready, t + 1)
                    pe.matmul(self_ps[:, 0:ROW], equal[:, :], tile_msg[:, :], start=True, stop=True).then_inc(merged, 1)

                pe_tile(0)
                with pe.Fori(1, EDGE_COLS) as t:
                    pe_tile(t)

        @block.gpsimd
        def _(pool):
            steps = Count(pool, pool_steps)
            pool.memset(w1_pair[:, :], 0.0).then_inc(zeros_set, 1)
            pool.memset(w1_self[:, :], 0.0).then_inc(zeros_set, 1)
            pool.memset(w4_pair[:, :], 0.0).then_inc(zeros_set, 1)
            pool.memset(base_row[:, :], 1.0).then_inc(zeros_set, 1)
            pool.iota(countdown[:, :], [[-1, EDGE_COLS]], base=KEY_TOP, channel_multiplier=0).then_inc(consts_set, 1)
            pool.iota(row_start[:, :], [[0, 1]], base=KEY_TOP, channel_multiplier=EDGE_COLS,
                      allow_small_or_imprecise_dtypes=True).then_inc(zeros_set, 1)
            pool.iota(minus_slot[:, :], [[-1, SLOTS]], base=0, channel_multiplier=0,
                      allow_small_or_imprecise_dtypes=True).then_inc(consts_set, 1)
            steps.up(pool.memset(ident[:, :], 0.0))
            steps.up(pool.memset(ones[:, :], 1.0))
            steps.settle()
            pool.affine_select(out=ident[:, :], in_=ident[:, :], compare_op=ALU.not_equal, fill=1.0, base=0,
                               pattern=[[-1, P]], channel_multiplier=1).then_inc(consts_set, 1)
            steps.up(pool.affine_select(out=before[:, :], in_=ones[:, :], compare_op=ALU.is_gt, fill=0.0, base=0,
                                        pattern=[[1, P]], channel_multiplier=-1))
            steps.up(pool.affine_select(out=earlier[:, :], in_=ones[:, :], compare_op=ALU.is_gt, fill=0.0, base=0,
                                        pattern=[[-1, P]], channel_multiplier=1))
            steps.settle()
            pool.drain().then_inc(consts_set, 1)

            marks = Count(pool, pool_marks)

            def hold(semaphore, value):
                if isinstance(value, int) and value <= 0:
                    return
                pool.wait_ge(semaphore, value)
                marks.settle()
                marks.up(pool.tensor_tensor(pool_mark[:, :], ones[:, 0:1], ones[:, 0:1], ALU.add))

            def merge_gather(number):
                hold(merge_asked, number)
                pool.indirect_dma_start(table_rows[:, :], None, table[:, :],
                                        bass.IndirectOffsetOnAxis(merge_index[:, 0:1], 0)).then_inc(merge_gathered, 16)

            def merge_scatter(number):
                hold(merge_rows_ready, number)
                pool.indirect_dma_start(table[:, :], bass.IndirectOffsetOnAxis(merge_out[:, 0:1], 0), new_rows[:, :], None,
                                        bounds_check=N - 1, oob_is_err=False).then_inc(merge_stored, 16)

            marks_before = marks.n
            way = take_way(pool)
            with pool.If(way == 1):
                def gather(pair, i, buf):
                    hold(slots_found, pair * 2 + i + 1)
                    hold(transposed, (pair - 2) * HALF_TILES + 2 + 2 * i + 1)
                    for s in range(TOP):
                        pool.indirect_dma_start(gathered[:, buf, s, 0:D], None, x[:, :],
                                                bass.IndirectOffsetOnAxis(dst_index[:, buf, s:s + 1], 0)
                                                ).then_inc(batch_gathered[buf], 16)
                        pool.indirect_dma_start(gathered[:, buf, s, D:2 * D], None, x[:, :],
                                                bass.IndirectOffsetOnAxis(src_index[:, buf, s:s + 1], 0)
                                                ).then_inc(batch_gathered[buf], 16)

                def scatter(pair, i, buf):
                    hold(rows_ready, pair * 2 + i + 1)
                    for s in range(TOP):
                        pool.indirect_dma_start(table[:, :], bass.IndirectOffsetOnAxis(out_index[:, buf, s:s + 1], 0),
                                                rows_out[:, buf, s, :], None, bounds_check=N - 1,
                                                oob_is_err=False).then_inc(rows_stored[buf], 16)

                PAIRS = BATCHES // 2
                for buf in range(4):
                    gather(buf // 2, buf % 2, buf)
                hold(table_started, 16 * (TABLE_PARTS + 1))
                start, built = marks.n, marks.built
                with pool.Fori(1, PAIRS // 2) as turn:
                    marks.n = (turn - 1) * TURN_MARKS + start
                    for buf in range(4):
                        scatter((turn - 1) * 2 + buf // 2, buf % 2, buf)
                        gather(turn * 2 + buf // 2, buf % 2, buf)
                assert marks.built == built + TURN_MARKS and PAIRS % 2 == 1
                marks.n = start + (PAIRS // 2 - 1) * TURN_MARKS
                for buf in range(2):
                    scatter(PAIRS - 3, buf, buf)
                    gather(PAIRS - 1, buf, buf)
                for pair in (PAIRS - 2, PAIRS - 1):
                    for i in range(2):
                        scatter(pair, i, pair % 2 * 2 + i)
                for buf in range(4):
                    hold(rows_stored[buf], 16 * TOP * len(range(buf, BATCHES, 4)))
                merge_gather(1)
                merge_scatter(1)
                hold(merge_stored, 16)
                pool.drain().then_inc(table_done, 1)
            with pool.If(way == 0):
                marks.n = marks_before
                pool.memset(self_msg[:, :, :], 0.0).then_inc(self_done, 1)
                hold(table_started, 16 * (TABLE_PARTS + 1))
                def pool_tile(t):
                    hold(merge_asked, t + 1)
                    pool.indirect_dma_start(tile_x[:, 0:D], None, x[:, :],
                                            bass.IndirectOffsetOnAxis(merge_index[:, 0:1], 0)).then_inc(tile_gathered, 16)
                    pool.indirect_dma_start(tile_x[:, D:2 * D], None, x[:, :],
                                            bass.IndirectOffsetOnAxis(merge_src[:, 0:1], 0)).then_inc(tile_gathered, 16)
                    hold(merge_stored, t * 16)
                    merge_gather(t + 1)
                    merge_scatter(t + 1)

                pool_tile(0)
                start, built = marks.n, marks.built
                with pool.Fori(1, EDGE_COLS) as t:
                    marks.n = (t - 1) * TILE_MARKS + start
                    pool_tile(t)
                assert marks.built == built + TILE_MARKS
                marks.n = start + (EDGE_COLS - 1) * TILE_MARKS
                hold(merge_stored, 16 * EDGE_COLS)
                pool.drain().then_inc(table_done, 1)

            pool.wait_ge(self_done, 1)

            def pool_last(b, i, round_):
                pool.wait_ge(last_loaded[i], round_ * 32 + 32)
                pool.tensor_tensor(sums[:, i, :, 0:D], sums[:, i, :, 0:D],
                                   self_msg[:, bass.ds(b, 1), :].rearrange("p b (c f) -> p (b c) f", f=D),
                                   ALU.add).then_inc(mean_added, 1)
                pool.wait_ge(share_ready, b + 1)
                pool.wait_ge(mean_added, b + 1)
                pool.tensor_tensor(sums[:, i, :, 0:D], sums[:, i, :, 0:D],
                                   share[:, i, :].unsqueeze(2).to_broadcast([P, NPP, D]), ALU.mult).then_inc(mean_ready, 1)

            for i in range(LAST_RING):
                pool_last(i, i, 0)
            with pool.Fori(1, FULL // LAST_RING) as turn:
                for i in range(LAST_RING):
                    pool_last(turn * LAST_RING + i, i, turn)
            pool_last(FULL, 0, FULL // LAST_RING)

        @block.vector
        def _(dve):
            steps = Count(dve, dve_steps)
            last_steps = Count(dve, dve_last_steps)

            def merge_start(column, number):
                dve.tensor_scalar(merge_index[:, :], column, float(N - 1), None, ALU.min).then_inc(merge_asked, 1)
                dve.tensor_scalar(dst_diag[:, :], ident[:, :], column, None, ALU.mult).then_inc(diag_ready, 1)

            def merge_equal(column, number):
                dve.wait_ge(dst_spread, number)
                dve.tensor_scalar(equal[:, :], t_ps[1][:, 0:P], column, None, ALU.is_equal).then_inc(equal_ready, 1)
                dve.wait_ge(equal_ready, number)
                steps.up(dve.tensor_tensor_reduce(equal_earlier[:, :], equal[:, :], earlier[:, :], 1.0, 0.0,
                                                  ALU.mult, ALU.add, repeats[:, :]))
                steps.settle()
                steps.up(dve.tensor_scalar(first_of[:, :], repeats[:, :], 0.0, None, ALU.is_equal))
                steps.up(dve.tensor_scalar(shifted[:, :], column, float(NOWHERE), None, ALU.subtract))
                steps.settle()
                steps.up(dve.tensor_tensor(first_of[:, :], first_of[:, :], shifted[:, :], ALU.mult))
                steps.settle()
                steps.up(dve.tensor_scalar(merge_out[:, :], first_of[:, :], float(NOWHERE), None, ALU.add))

            def merge_finish(totals, number):
                dve.wait_ge(merged, number)
                dve.wait_ge(merge_gathered, number * 16)
                steps.settle()
                dve.tensor_tensor(new_rows[:, :], table_rows[:, :], totals, ALU.add).then_inc(merge_rows_ready, 1)

            dve.memset(dst_sb[96:P, LAST_COLS:EDGE_COLS], NOWHERE).then_inc(pads_set, 1)
            dve.memset(nxt_sb[96:P, LAST_COLS - 1:EDGE_COLS], NOWHERE).then_inc(pads_set, 1)
            dve.memset(src_sb[96:P, LAST_COLS:EDGE_COLS], 0).then_inc(pads_set, 1)
            dve.memset(msg[:, :, :], 1.0).then_inc(dve_set, 1)
            dve.memset(same_run[:, :, :], 0.0).then_inc(dve_set, 1)
            dve.memset(run_sum[:, :, :], 0.0).then_inc(dve_set, 1)
            dve.memset(first_sum[:, :], 0.0).then_inc(dve_set, 1)
            dve.memset(tile_msg[:, :], 1.0).then_inc(dve_set, 1)
            dve.memset(eps[:, :], EPS).then_inc(dve_set, 1)
            dve.memset(tile_x[:, 2 * D:4 * D], 0.0).then_inc(dve_set, 1)
            dve.memset(dst_of_slot[:, 0:1], -1.0).then_inc(dve_set, 1)
            dve.memset(dst_of_slot[:, SLOTS + 1:SLOTS + 2], float(NOWHERE)).then_inc(dve_set, 1)
            dve.wait_ge(edges_in, 16 * EDGE_LOADS)
            steps.up(dve.tensor_tensor(work_a[:, :], src_sb[:, :], dst_sb[:, :], ALU.is_equal))
            steps.up(dve.tensor_tensor(work_b[:, :], nxt_sb[:, :], dst_sb[:, :], ALU.not_equal))
            steps.settle()
            steps.up(dve.tensor_tensor_reduce(work_a[:, :], work_a[:, :], work_b[:, :], 1.0, 0.0,
                                              ALU.mult, ALU.add, stats[:, 0:1]))
            steps.settle()
            steps.up(dve.tensor_tensor_reduce(work_b[:, :], dst_sb[:, :], nxt_sb[:, :], 1.0, 0.0,
                                              ALU.subtract, ALU.max, largest_fall[:, :]))
            steps.up(dve.scalar_tensor_tensor(out=extra[:, :], in0=dst_sb[:, :], scalar=float(NOWHERE), in1=work_a[:, :],
                                              op0=ALU.is_lt, op1=ALU.subtract, accum_out=extras_in_row[:, :]))
            steps.settle()
            steps.up(dve.tensor_scalar(stats[:, 1:2], largest_fall[:, :], 0.0, None, ALU.is_gt))
            steps.up(dve.tensor_scalar(stats[:, 2:3], extras_in_row[:, :], float(SLOTS), None, ALU.is_gt))
            steps.settle()
            dve.drain().then_inc(stats_ready, 1)
            dve.wait_ge(consts_set, 4)
            steps.up(dve.tensor_tensor(key[:, :], extra[:, :], countdown[:, :], ALU.mult))
            steps.up(dve.tensor_tensor(nxt_sb[:, :], extra[:, :], src_sb[:, :], ALU.mult))
            steps.settle()
            steps.up(dve.tensor_scalar(key[:, :], key[:, :], SRC_BITS, None, ALU.logical_shift_left))
            steps.settle()
            steps.up(dve.tensor_tensor(key[:, :], key[:, :], nxt_sb[:, :], ALU.bitwise_or))
            dve.wait_ge(totals_ready, 1)
            dve.wait_ge(zeros_set, 5)
            steps.up(dve.tensor_scalar(checks[:, 0:1], extra_ps[:, 0:1], float(N), None, ALU.is_equal))
            steps.up(dve.tensor_scalar(checks[:, 1:3], extra_ps[:, 1:3], 0.0, None, ALU.is_equal))
            steps.up(dve.tensor_tensor(node_base[:, :], row_start[:, :], extra_ps[:, 4:5], ALU.subtract))
            steps.settle()
            steps.up(dve.tensor_tensor(flag_f[:, :], checks[:, 0:1], checks[:, 1:2], ALU.mult))
            steps.settle()
            steps.up(dve.tensor_tensor(flag_f[:, :], flag_f[:, :], checks[:, 2:3], ALU.mult))
            steps.up(dve.tensor_scalar(slot_base[:, :], minus_slot[:, :], node_base[:, 0:1], None, ALU.add))
            steps.settle()
            dve.tensor_copy(flag[:, :], flag_f[:, :]).then_inc(flag_ready, 1)
            dve.wait_ge(weights_in, 16 * (WEIGHT_LOADS - 1))
            steps.up(dve.tensor_reduce(w4_sum[:, 0:1], w4_pair[:, :], AX.X, ALU.add))
            steps.up(dve.tensor_reduce(w4_sum[:, 1:2], base_row[:, 0:D], AX.X, ALU.add))
            steps.settle()
            steps.up(dve.tensor_scalar(w4_mean[:, :], w4_sum[:, :], 1.0 / D, None, ALU.mult))
            steps.settle()
            steps.up(dve.tensor_scalar(base_row[:, 0:D], base_row[:, 0:D], w4_mean[:, 1:2], None, ALU.subtract))
            for h in (0, 1):
                dve.tensor_scalar(w4_pair[64 * h:64 * h + 64, D * h:D * h + D], w4_pair[64 * h:64 * h + 64, D * h:D * h + D],
                                  w4_mean[64 * h:64 * h + 64, 0:1], None, ALU.subtract).then_inc(w4_ready, 1)
            steps.settle()
            dve.tensor_scalar(base_tile[:, :, :], base_row[:, :].unsqueeze(1).to_broadcast([P, NPP, ROW]),
                              flag_f[:, 0:1], None, ALU.mult).then_inc(base_ready, 1)
            dve.wait_ge(dve_set, 9)

            def centre(b, ring, rounds):
                dve.wait_ge(x_loaded[ring], rounds * 16 + 16)
                rows = x_in[:, ring, :].rearrange("p (c f) -> p c f", f=D)
                steps.settle()
                steps.up(dve.tensor_reduce(x_sum[:, :], rows, AX.X, ALU.add))
                steps.settle()
                steps.up(dve.tensor_scalar(x_mean[:, :], x_sum[:, :], 1.0 / D, None, ALU.mult))
                steps.settle()
                wait(dve, centred_made, b)
                wait(dve, centred_stored[ring], rounds * 16)
                dve.tensor_tensor(x_mid[:, ring, :].rearrange("p (c f) -> p c f", f=D), rows,
                                  x_mean[:, :].unsqueeze(2).to_broadcast([P, NPP, D]), ALU.subtract).then_inc(centred_made, 1)

            def search(pair, i, buf, lap):
                steps.settle()
                steps.up(dve.memset(mark[:, :], 0.0))
                steps.up(dve.max(out=top[:, :], in_=key_f))
                steps.settle()
                steps.up(dve.memset(mark[:, :], 0.0))
                steps.up(dve.match_replace(out=key_f, in_to_replace=top[:, :], in_values=key_f, imm_value=0.0))
                wait(dve, batch_gathered[buf], lap * (16 * 2 * TOP))
                steps.up(dve.tensor_scalar(src_index[:, buf, :], top_bits, (1 << SRC_BITS) - 1, None, ALU.bitwise_and))
                steps.up(dve.tensor_scalar(key_count[:, :], top_bits, SRC_BITS, None, ALU.logical_shift_right))
                steps.settle()
                steps.up(dve.tensor_scalar(found[:, :], key_count[:, :], 0.0, None, ALU.is_gt))
                steps.up(dve.tensor_tensor(slot_dst[:, :], slot_base[:, bass.ds(pair * (2 * TOP) + i * TOP, TOP)],
                                           key_count[:, :], ALU.subtract))
                steps.settle()
                steps.up(dve.tensor_tensor(dst_index[:, buf, :], slot_dst[:, :], found[:, :], ALU.mult))
                steps.up(dve.scalar_tensor_tensor(out=slot_dst[:, :], in0=slot_dst[:, :], scalar=float(NOWHERE),
                                                  in1=found[:, :], op0=ALU.subtract, op1=ALU.mult))
                steps.settle()
                dve.tensor_scalar(dst_of_slot[:, bass.ds(pair * (2 * TOP) + i * TOP + 1, TOP)], slot_dst[:, :],
                                  float(NOWHERE), None, ALU.add).then_inc(slots_found, 1)

            def difference(buf, lap):
                dve.wait_ge(batch_gathered[buf], lap * (16 * 2 * TOP) + 16 * 2 * TOP)
                dve.tensor_tensor(gathered[:, buf, :, D:2 * D], gathered[:, buf, :, D:2 * D], gathered[:, buf, :, 0:D],
                                  ALU.subtract).then_inc(difference_ready, 1)

            def runs(pair, i, buf, lap, last=False):
                here = dst_of_slot[:, bass.ds(pair * (2 * TOP) + i * TOP + 1, TOP)]
                left = dst_of_slot[:, bass.ds(pair * (2 * TOP) + i * TOP, TOP)]
                right = dst_of_slot[:, bass.ds(pair * (2 * TOP) + i * TOP + 2, TOP)]
                steps.settle()
                wait(dve, rows_ready, pair * 2 + i)
                steps.up(dve.tensor_copy(msg[:, :, 0:1], run_sum[:, :, TOP:TOP + 1]))
                dve.wait_ge(slots_found, BATCHES if last else pair * 2 + i + 2)
                steps.up(dve.tensor_tensor(same_run[:, :, 1:TOP + 1], here.unsqueeze(1).to_broadcast([P, ROW, TOP]),
                                           left.unsqueeze(1).to_broadcast([P, ROW, TOP]), ALU.is_equal))
                steps.up(dve.tensor_scalar(is_first[:, :], here, dst_of_slot[:, 1:2], None, ALU.is_equal))
                steps.up(dve.tensor_scalar(not_first[:, :], here, dst_of_slot[:, 1:2], None, ALU.not_equal))
                steps.up(dve.tensor_tensor(run_end[:, :], here, right, ALU.not_equal))
                dve.wait_ge(msg_done, pair * HALF_LEN + HALF_TURN.index("X") + 3 * i + 1)
                dve.tensor_tensor(msg[:, 0:D, 1:TOP + 1], extra_ps[:, 0:TOP * D].rearrange("p (s f) -> p f s", f=D),
                                  base_row[:, 0:D].unsqueeze(2).to_broadcast([P, D, TOP]), ALU.add).then_inc(extras_taken, 1)
                dve.wait_ge(extras_taken, pair * 2 + i + 1)
                steps.settle()
                steps.up(dve.tensor_tensor_scan(run_sum[:, :, :].rearrange("p f s -> p (f s)"),
                                                same_run[:, :, :].rearrange("p f s -> p (f s)"),
                                                msg[:, :, :].rearrange("p f s -> p (f s)"), 0.0, ALU.mult, ALU.add))
                steps.up(dve.tensor_tensor(first_part[:, :, :], msg[:, :, 1:TOP + 1],
                                           is_first[:, :].unsqueeze(1).to_broadcast([P, ROW, TOP]), ALU.mult))
                steps.up(dve.tensor_tensor(run_end[:, :], run_end[:, :], not_first[:, :], ALU.mult))
                steps.settle()
                steps.up(dve.tensor_reduce(first_add[:, :], first_part[:, :, :], AX.X, ALU.add))
                steps.up(dve.scalar_tensor_tensor(out=run_end[:, :], in0=here, scalar=float(NOWHERE), in1=run_end[:, :],
                                                  op0=ALU.subtract, op1=ALU.mult))
                wait(dve, rows_stored[buf], lap * (16 * TOP))
                steps.up(dve.tensor_tensor(rows_out[:, buf, :, :], run_sum[:, :, 1:TOP + 1].rearrange("p f s -> p s f"),
                                           base_row[:, :].unsqueeze(1).to_broadcast([P, TOP, ROW]), ALU.add))
                steps.settle()
                steps.up(dve.tensor_tensor(first_sum[:, :], first_sum[:, :], first_add[:, :], ALU.add))
                dve.tensor_scalar(out_index[:, buf, :], run_end[:, :], float(NOWHERE), None, ALU.add).then_inc(rows_ready, 1)

            before_ways = steps.n
            way = take_way(dve)
            with dve.If(way == 1):
                PAIRS = BATCHES // 2

                def one_pair(pair, lap, odd, further=True):
                    next_lap, there = (lap + 1, 0) if odd else (lap, 2)
                    for i in range(2):
                        runs(pair, i, 2 * odd + i, lap)
                        for r in ((0, 1), (2,))[i]:
                            centre((pair + 1) * RING + r, r, pair + 1)
                        difference(there + i, next_lap)
                        if further:
                            search(pair + 3, i, there + i, next_lap + 1)

                for buf in range(4):
                    search(buf // 2, buf % 2, buf, 0)
                for i in range(2):
                    for r in ((0, 1), (2,))[i]:
                        centre(r, r, 0)
                    difference(i, 0)
                    search(2, i, i, 1)
                for pair in range(3):
                    one_pair(pair, pair // 2, pair % 2)
                start, built = steps.n, steps.built
                with dve.Fori(1, (PAIRS - 3) // 2 - 1) as turn:
                    steps.n = (turn - 1) * CHAIN_STEPS + start
                    one_pair(turn * 2 + 1, turn, 1)
                    one_pair(turn * 2 + 2, turn + 1, 0)
                assert steps.built == built + CHAIN_STEPS
                steps.n = start + ((PAIRS - 3) // 2 - 2) * CHAIN_STEPS
                for pair in range(2 * ((PAIRS - 3) // 2) - 1, PAIRS - 1):
                    one_pair(pair, pair // 2, pair % 2, further=pair + 3 < PAIRS)
                pair = PAIRS - 1
                left = list(range(PAIRS * RING, BLOCKS))
                for i in range(2):
                    runs(pair, i, pair % 2 * 2 + i, pair // 2, last=i == 1)
                    for b in left[2 * i:2 * i + 2]:
                        centre(b, b % RING, b // RING)
                steps.settle()
                merge_start(dst_of_slot[:, 1:2], 1)
                merge_equal(dst_of_slot[:, 1:2], 1)
                merge_finish(extra_ps[:, 256:256 + ROW], 1)
            with dve.If(way == 0):
                dve.wait_ge(base_ready, 1)
                steps.n = before_ways
                for r in range(RING):
                    centre(r, r, 0)
                start, built = steps.n, steps.built
                with dve.Fori(1, FULL // RING) as half:
                    steps.n = (half - 1) * (2 * RING) + start
                    for r in range(RING):
                        centre(half * RING + r, r, half)
                assert steps.built == built + 2 * RING
                steps.n = start + (FULL // RING - 1) * (2 * RING)
                centre(FULL, FULL % RING, FULL // RING)

                def dve_tile(t):
                    steps.settle()
                    wait(dve, merge_stored, t * 16)
                    steps.up(dve.tensor_copy(merge_dst[:, :], dst_sb[:, bass.ds(t, 1)]))
                    steps.up(dve.tensor_copy(merge_src[:, :], src_sb[:, bass.ds(t, 1)]))
                    steps.settle()
                    merge_start(merge_dst[:, 0:1], t + 1)
                    dve.wait_ge(tile_gathered, t * 32 + 32)
                    dve.tensor_tensor(tile_x[:, D:2 * D], tile_x[:, D:2 * D], tile_x[:, 0:D], ALU.subtract).then_inc(tile_diff, 1)
                    merge_equal(merge_dst[:, 0:1], t + 1)
                    dve.wait_ge(tile_pe, t * 7 + 7)
                    dve.tensor_tensor(tile_msg[:, 0:D], extra_ps[:, 0:D], base_row[:, 0:D], ALU.add).then_inc(tile_msg_ready, 1)
                    merge_finish(self_ps[:, 0:ROW], t + 1)

                dve_tile(0)
                start, built = steps.n, steps.built
                with dve.Fori(1, EDGE_COLS) as t:
                    steps.n = (t - 1) * MERGE_STEPS + start
                    dve_tile(t)
                assert steps.built == built + MERGE_STEPS

            def find_share(b, i, rounds):
                dve.wait_ge(last_loaded[i], rounds * 32 + 32)
                last_steps.up(dve.tensor_scalar(counts[:, i, :], sums[:, i, :, D], 1.0, None, ALU.max))
                last_steps.settle()
                dve.reciprocal(share[:, i, :], counts[:, i, :]).then_inc(share_ready, 1)

            def dve_last(b, i, next_rounds, old_rounds):
                inside = not isinstance(b, int)
                if inside or b + 1 < BLOCKS:
                    find_share(b + 1, (i + 1) % LAST_RING, next_rounds)
                if inside or b < BLOCKS:
                    dve.wait_ge(mean_ready, b + 1)
                    wait(dve, result_ready, b - LAST_RING + 1)
                    dve.tensor_tensor(y[:, i, :, :], x_last[:, i, :, :], sums[:, i, :, 0:D], ALU.add).then_inc(y_ready, 1)
                if inside or 1 <= b <= BLOCKS:
                    j = (i - 1) % LAST_RING
                    dve.wait_ge(square_ready, b)
                    wait(dve, std_ready, b - LAST_RING)
                    dve.tensor_reduce(square_sum[:, j, :], square[:, j % 2, :, :], AX.X, ALU.add).then_inc(square_summed, 1)
                if inside or 2 <= b:
                    j = (i - 2) % LAST_RING
                    dve.wait_ge(std_ready, b - 1)
                    wait(dve, result_ready, b - 2)
                    last_steps.up(dve.reciprocal(rstd, std[:, j, :]))
                    last_steps.settle()
                    wait(dve, result_stored[j], old_rounds * 16)
                    dve.tensor_tensor(result[:, j, :, :], y[:, j, :, :],
                                      rstd.unsqueeze(2).to_broadcast([P, NPP, D]), ALU.mult).then_inc(result_ready, 1)

            find_share(0, 0, 0)
            for b in range(2 * LAST_RING):
                dve_last(b, b % LAST_RING, (b + 1) // LAST_RING, (b - 2) // LAST_RING)
            start, built = last_steps.n, last_steps.built
            with dve.Fori(2, FULL // LAST_RING) as turn:
                last_steps.n = (turn - 2) * LAST_STEPS + start
                for i in range(LAST_RING):
                    dve_last(turn * LAST_RING + i, i, turn + 1 if i == LAST_RING - 1 else turn, turn if i >= 2 else turn - 1)
            assert last_steps.built == built + LAST_STEPS
            last_steps.n = start + (FULL // LAST_RING - 2) * LAST_STEPS
            for b in range(FULL, BLOCKS + 2):
                dve_last(b, b % LAST_RING, (b + 1) // LAST_RING, (b - 2) // LAST_RING)


_INS = ["x", "src", "dst", "L0_gnn_W1", "L0_gnn_b1", "L0_gnn_W2", "L0_gnn_b2", "L0_gnn_W3", "L0_gnn_b3",
        "L0_gnn_W4", "L0_gnn_b4"]


def kernel(**inputs):
    import numpy as np
    import concourse.bacc as bacc
    from concourse.bass_utils import run_bass_kernel_spmd

    nc = bacc.Bacc("TRN2", target_bir_lowering=False, num_devices=1)
    arrays, args = {}, []
    for name in _INS:
        a = np.ascontiguousarray(inputs[name])
        arrays[f"in_{name}"] = a
        args.append(nc.dram_tensor(f"in_{name}", a.shape, mybir.dt.from_np(a.dtype), kind="ExternalInput").ap())
    out = nc.dram_tensor("out_0", arrays["in_x"].shape, F32, kind="ExternalOutput").ap()
    gnn_program(nc, *args, out)
    r = run_bass_kernel_spmd(nc, [arrays], core_ids=[0])
    return r.results[0]["out_0"]
```

```python
import concourse.bass as bass
from concourse import mybir
from contextlib import ExitStack

F32 = mybir.dt.float32
I32 = mybir.dt.int32
ALU = mybir.AluOpType
ACT = mybir.ActivationFunctionType
AX = mybir.AxisListType

P = 128
EPS = 1e-5
NOWHERE = 1 << 20
SRC_BITS = 17
TOP = 8


def wait(eng, sem, value):
    if isinstance(value, int) and value <= 0:
        return
    eng.wait_ge(sem, value)


class Count:

    def __init__(self, eng, sem):
        self.eng, self.sem, self.n = eng, sem, 0
        self.built = 0

    def up(self, instruction):
        instruction.then_inc(self.sem, 1)
        self.n = self.n + 1
        self.built += 1

    def settle(self, n=None):
        wait(self.eng, self.sem, self.n if n is None else n)


def gnn_program(nc, x, src, dst, W1, b1, W2, b2, W3, b3, W4, b4, out):
    N, D = x.shape
    E = src.shape[0]
    H1, H2, H3 = W1.shape[1], W2.shape[1], W3.shape[1]
    ROW = D + 1
    assert (2 * D, H1, H2, H3, W4.shape[1]) == (64, 64, 128, 64, 32) and N < 1 << SRC_BITS

    EDGE_COLS = -(-E // P)
    LAST_COLS = E - (P - 1) * EDGE_COLS
    SLOTS = 240
    BATCHES = SLOTS // TOP
    MERGE_STEPS = 2 + 5
    SEARCH_STEPS, RUNS_STEPS, FINISH_STEPS, BLOCK_STEPS = 10, 16, 1, 5
    LAST_STEPS = 9
    TILE_MARKS = 4
    KEY_TOP = 2048 + EDGE_COLS

    NPP = 16
    BLOCK = P * NPP
    FULL = N // BLOCK
    REST = (N - FULL * BLOCK) // NPP
    BLOCKS = FULL + 1
    assert 0 < REST < P and (N - FULL * BLOCK) % NPP == 0

    RING = 7
    BLOCK_TURNS = BLOCKS // RING
    LANDINGS = 4
    EARLY = 1
    PLAIN_TURNS = BLOCK_TURNS - EARLY
    PAIR_TURNS = (BATCHES - EARLY - 3) // 2
    SECTIONS = [("AB" * RING, PLAIN_TURNS), ("AB" * RING + "XS", EARLY), ("XSXSXS", 1), ("XSXS", PAIR_TURNS)]
    UNITS = "".join(pattern * turns for pattern, turns in SECTIONS)
    assert BLOCKS % RING == 0 and UNITS.count("A") == BLOCKS and UNITS.count("X") == BATCHES
    COUNTED = range(len(UNITS))
    TILE_OF = [sum(k in "AX" for k in UNITS[:u + 1]) - 1 for u in COUNTED]
    BLOCK_OF = [UNITS[:u + 1].count("A") - 1 for u in COUNTED]
    BATCH_OF = [UNITS[:u + 1].count("X") - 1 for u in COUNTED]
    ROUND_OF = [b // RING for b in BLOCK_OF]
    BUFFER_OF_BATCH = [0] * EARLY + [(b - EARLY + 1) % 2 for b in range(EARLY, BATCHES)]
    TILE_OF_BATCH = [TILE_OF[u] for u in COUNTED if UNITS[u] == "X"]
    X_AT = [u for u in COUNTED if UNITS[u] == "X"]
    TILE_BUFFER = [BLOCK_OF[u] % RING % 2 if UNITS[u] in "AB" else
                   1 if BATCH_OF[u] < EARLY else (BATCH_OF[u] - EARLY) % 2 for u in COUNTED]
    USERS_BEFORE = [[v for v in range(u) if TILE_BUFFER[v] == TILE_BUFFER[u] and TILE_OF[v] < TILE_OF[u]] for u in COUNTED]
    COPIED_AT = [TILE_OF[before[-1]] + 1 if before else 0 for before in USERS_BEFORE]
    FREE_AT = [before[-1] + 1 if before else 0 for before in USERS_BEFORE]
    NORM_AT = [BLOCK_OF[u] if UNITS[u] == "A" else u - X_AT[EARLY] + BLOCKS
               if 0 <= u - X_AT[EARLY] < 6 else -1 for u in COUNTED]
    SHORT = len(UNITS) - 4
    SQUARE_LAG, ROOT_LAG = 4, 6
    SUM_LAG, RESULT_LAG = 2, 4

    class Step:

        def __init__(self, ref, length=0, on=None, end=len(UNITS)):
            self.ref, self.length, self.on, self.end = ref, length, on, end

        def has(self, shift=0):
            return 0 <= self.ref + shift < self.end

        def kind(self, shift=0):
            return UNITS[self.ref + shift]

        def of(self, numbers, shift=0):
            n = numbers[self.ref + shift]
            return n if self.on is None else self.on * (numbers[self.ref + shift + self.length] - n) + n

        def place(self, numbers, ring, shift=0):
            return numbers[self.ref + shift] % ring

    def run_steps(eng, step):
        start = 0
        for pattern, turns in SECTIONS:
            length = len(pattern)
            end = start + turns * length
            if turns > 3:
                for u in range(start, start + length):
                    step(Step(u))
                with eng.Fori(1, turns - 1) as turn:
                    for u in range(start + length, start + 2 * length):
                        step(Step(u, length, turn - 1))
                start = end - length
            for u in range(start, min(end, SHORT)):
                step(Step(u))
            start = end

    def run_last_steps(step, last):
        for u in range(SHORT, last + 3):
            step(Step(u, end=last))

    table = nc.dram_tensor("sums_of_messages", (N, ROW), F32).ap()
    x_blocks = x[0:FULL * BLOCK, :].rearrange("(b p c) f -> b p (c f)", p=P, c=NPP)
    x_rest = x[FULL * BLOCK:N, :].rearrange("(p c) f -> p (c f)", c=NPP)
    out_blocks = out[0:FULL * BLOCK, :].rearrange("(b p c) f -> b p (c f)", p=P, c=NPP)
    out_rest = out[FULL * BLOCK:N, :].rearrange("(p c) f -> p (c f)", c=NPP)
    table_blocks = table[0:FULL * BLOCK, :].rearrange("(b p c) f -> b p (c f)", p=P, c=NPP)
    table_rest = table[FULL * BLOCK:N, :].rearrange("(p c) f -> p (c f)", c=NPP)

    with ExitStack() as ctx:
        def sb(name, shape, dt=F32):
            return ctx.enter_context(nc.sbuf_tensor(name, shape, dt))

        def sem(name):
            return ctx.enter_context(nc.semaphore(name))

        src_sb = sb("src_sb", [P, EDGE_COLS], I32)
        dst_sb = sb("dst_sb", [P, EDGE_COLS], I32)
        nxt_sb = sb("nxt_sb", [P, EDGE_COLS], I32)
        key = sb("key", [P, EDGE_COLS], I32)
        key_f = key[:, :].bitcast(F32)
        scratch = sb("scratch", [P, 4, EDGE_COLS])
        work_a, work_b, extra = scratch[:, 0, :], scratch[:, 1, :], scratch[:, 2, :]
        countdown = scratch[:, 3, :].bitcast(I32)

        ident = sb("ident", [P, P])
        ones = sb("ones", [P, P])
        before = sb("before", [P, P])
        earlier = sb("earlier", [P, P])
        w1_pair = sb("w1_pair", [P, P])
        w1_self = sb("w1_self", [P, P])
        w1_slot = sb("w1_slot", [P, P])
        w2_twice = sb("w2_twice", [P, P])
        w3_sb = sb("w3_sb", [P, H3])
        w4_pair = sb("w4_pair", [P, 2 * D])
        b1_sb = sb("b1_sb", [P, 1])
        b2_sb = sb("b2_sb", [P, 1])
        b3_sb = sb("b3_sb", [P, 1])
        base_row = sb("base_row", [P, ROW])
        eps = sb("eps", [P, 1])

        stats = sb("stats", [P, 4])
        largest_fall = sb("largest_fall", [P, 1])
        extras_in_row = sb("extras_in_row", [P, 1])
        checks = sb("checks", [P, 3])
        flag_f = sb("flag_f", [P, 1])
        flag = sb("flag", [P, 1], I32)
        long_f = sb("long_f", [P, 1])
        long_flag = sb("long_flag", [P, 1], I32)
        row_start = sb("row_start", [P, 1])
        node_base = sb("node_base", [P, 1])
        minus_slot = sb("minus_slot", [P, SLOTS])
        slot_base = sb("slot_base", [P, SLOTS])

        top = sb("top", [P, TOP])
        top_bits = top[:, :].bitcast(I32)
        mark = sb("mark", [P, 1])
        pool_mark = sb("pool_mark", [P, 1])
        key_count = sb("key_count", [P, TOP], I32)
        found = sb("found", [P, TOP])
        slot_dst = sb("slot_dst", [P, TOP])
        dst_of_slot = sb("dst_of_slot", [P, SLOTS + 2])
        last_dst = sb("last_dst", [P, 1])
        ends_index = sb("ends_index", [P, BATCHES, 2, TOP], I32)
        out_index = sb("out_index", [P, SLOTS], I32)
        ends_now = sb("ends_now", [P, LANDINGS, 2, TOP], I32)
        out_now = sb("out_now", [P, 2, TOP], I32)
        gathered = sb("gathered", [P, LANDINGS, TOP, 2 * D])
        kept = sb("kept", [P, BATCHES, TOP, 2 * D])
        x_pair = sb("x_pair", [P, 2, TOP, 2 * D])
        x_in = sb("x_in", [P, RING, NPP * D])
        self_msg = scratch[:, :, :].rearrange("p a n -> p (a n)")[:, 0:RING * NPP * D].rearrange(
            "p (r n) -> p r n", r=RING)
        y = sb("y", [P, RING, NPP, D])
        y_sum = sb("y_sum", [P, NPP])
        y_mean = sb("y_mean", [P, NPP])
        square = sb("square", [P, 2, NPP, D])
        square_sum = sb("square_sum", [P, RING, NPP])
        std = sb("std", [P, RING, NPP])
        rstd = sb("rstd", [P, NPP])
        xT = sb("xT", [P, 2, 512])
        h1 = sb("h1", [P, 2, 512])
        h2 = sb("h2", [P, 2, 2, 512])
        h3 = sb("h3", [P, 2, 512])
        msg = sb("msg", [P, ROW, TOP + 1])
        same_run = sb("same_run", [P, BATCHES, TOP + 1])
        run_sum = sb("run_sum", [P, ROW, TOP + 1])
        part = sb("part", [P, 2, ROW, TOP])
        part_add = sb("part_add", [P, 2, ROW])
        part_sum = sb("part_sum", [P, 2, ROW])
        part_mask = sb("part_mask", [P, 2, SLOTS])
        go_on = sb("go_on", [P, ROW, TOP + 1])
        run_end = sb("run_end", [P, SLOTS])
        not_first = sb("not_first", [P, SLOTS])
        slot_count = sb("slot_count", [P, TOP])
        slot_share = sb("slot_share", [P, TOP])
        slot_msg = sb("slot_msg", [P, TOP, D])
        slot_x = sb("slot_x", [P, TOP, D])
        slot_sum = sb("slot_sum", [P, TOP])
        slot_mean = sb("slot_mean", [P, TOP])
        slot_square = sb("slot_square", [P, TOP, D])
        slot_rstd = sb("slot_rstd", [P, TOP])
        slot_square_sum = sb("slot_square_sum", [P, SLOTS])
        slot_std = sb("slot_std", [P, SLOTS])
        first_x = sb("first_x", [P, D])
        first_self = sb("first_self", [P, D])
        rows_now = sb("rows_now", [P, 2, TOP, D])

        merge_dst = sb("merge_dst", [P, 1])
        merge_index = sb("merge_index", [P, 1], I32)
        merge_out = sb("merge_out", [P, 1], I32)
        merge_src = sb("merge_src", [P, 1], I32)
        dst_diag = sb("dst_diag", [P, P])
        equal = sb("equal", [P, P])
        equal_earlier = sb("equal_earlier", [P, P])
        repeats = sb("repeats", [P, 1])
        shifted = sb("shifted", [P, 1])
        first_of = sb("first_of", [P, 1])
        table_rows = sb("table_rows", [P, ROW])
        new_rows = sb("new_rows", [P, ROW])
        tile_msg = sb("tile_msg", [P, ROW])
        tile_x = sb("tile_x", [P, 4 * D])

        equal_last = sb("equal_last", [P, P])
        end_x = sb("end_x", [P, NPP, D])
        end_sums = kept[:, 0:2, :, :].rearrange("p b s f -> p (b s f)")[:, 0:NPP * ROW].rearrange(
            "p (c f) -> p c f", f=ROW)
        end_y = kept[:, 2, :, :].rearrange("p s f -> p (s f)").rearrange("p (c f) -> p c f", f=D)
        end_square = kept[:, 3, :, :].rearrange("p s f -> p (s f)").rearrange("p (c f) -> p c f", f=D)
        zero_rows = kept[:, 4:6, :, :].rearrange("p b s f -> p (b s f)")[:, 0:NPP * ROW]
        end_count = sb("end_count", [P, NPP])
        end_mean = sb("end_mean", [P, NPP])
        end_std = sb("end_std", [P, NPP])
        end_row = sb("end_row", [P, D])

        def bank(name):
            return ctx.enter_context(nc.psum_tensor(name, [P, 512], F32))

        t_ps = [bank("t_ps0"), bank("t_ps1")]
        h1_ps, h2a_ps, h2b_ps, h3_ps = bank("h1_ps"), bank("h2a_ps"), bank("h2b_ps"), bank("h3_ps")
        self_ps, extra_ps = bank("self_ps"), bank("extra_ps")
        h2_ps = [h2a_ps, h2b_ps]

        pads_set = sem("pads_set")
        edges_in = sem("edges_in")
        zeros_set = sem("zeros_set")
        dve_set = sem("dve_set")
        weights_in = sem("weights_in")
        consts_set = sem("consts_set")
        pool_steps = sem("pool_steps")
        pool_marks = sem("pool_marks")
        dve_steps = sem("dve_steps")
        dve_end_steps = sem("dve_end_steps")
        stats_ready = sem("stats_ready")
        totals_ready = sem("totals_ready")
        flag_ready = sem("flag_ready")
        table_started = sem("table_started")

        x_loaded = [sem(f"x_loaded{i}") for i in range(RING)]
        slots_found = sem("slots_found")
        batch_gathered = [sem(f"batch_gathered{i}") for i in range(LANDINGS)]
        batch_kept = sem("batch_kept")
        pair_ready = sem("pair_ready")
        transposed = sem("transposed")
        xT_ready = sem("xT_ready")
        h1_done, h1_ready = sem("h1_done"), sem("h1_ready")
        h2_done, h2_ready = sem("h2_done"), sem("h2_ready")
        h3_done, h3_ready = sem("h3_done"), sem("h3_ready")
        msg_done = sem("msg_done")
        self_stored = sem("self_stored")
        y_begun = sem("y_begun")
        y_ready = sem("y_ready")
        square_ready = sem("square_ready")
        square_summed = sem("square_summed")
        std_ready = sem("std_ready")
        result_ready = sem("result_ready")
        result_stored = [sem(f"result_stored{i}") for i in range(RING)]
        extras_taken = sem("extras_taken")
        slot_sums_ready = sem("slot_sums_ready")
        slot_std_ready = sem("slot_std_ready")
        rows_ready = sem("rows_ready")
        rows_stored = [sem(f"rows_stored{i}") for i in range(2)]

        merge_asked = sem("merge_asked")
        diag_ready = sem("diag_ready")
        dst_spread = sem("dst_spread")
        equal_ready = sem("equal_ready")
        merged = sem("merged")
        merge_gathered = sem("merge_gathered")
        merge_rows_ready = sem("merge_rows_ready")
        merge_stored = sem("merge_stored")
        tile_gathered = sem("tile_gathered")
        tile_diff = sem("tile_diff")
        tile_pe = sem("tile_pe")
        tile_act = sem("tile_act")
        tile_msg_ready = sem("tile_msg_ready")

        table_done = sem("table_done")
        end_loaded = sem("end_loaded")
        end_summed = sem("end_summed")
        end_std_ready = sem("end_std_ready")
        end_ready = sem("end_ready")
        end_stored = sem("end_stored")

        WEIGHT_LOADS = 19
        EDGE_LOADS = 9
        SPLIT = (P - 1) // 16 * 16

        DVE_SETS = 10
        EVERY = list(COUNTED)

        def take_way(eng):
            eng.wait_ge(flag_ready, 2)
            return eng.value_load(flag[0:1, 0:1], min_val=0, max_val=1)

        def take_long(eng):
            return eng.value_load(long_flag[0:1, 0:1], min_val=0, max_val=1)

        block = ctx.enter_context(nc.Block())

        @block.sync
        def _(sp):
            sp.wait_ge(pads_set, 3)
            for tile, flat, n in ((dst_sb, dst, E), (nxt_sb, dst[1:E], E - 1), (src_sb, src, E)):
                for lo, hi in ((0, SPLIT), (SPLIT, P - 1)):
                    sp.dma_start(tile[lo:hi, :], flat[lo * EDGE_COLS:hi * EDGE_COLS].rearrange(
                        "(p c) -> p c", c=EDGE_COLS)).then_inc(edges_in, 16)
                cols = n - (P - 1) * EDGE_COLS
                sp.dma_start(tile[P - 1:P, 0:cols], flat[(P - 1) * EDGE_COLS:n].rearrange(
                    "(p c) -> p c", p=1)).then_inc(edges_in, 16)

            def load_block(b, ring):
                wait(sp, y_begun, b - RING + 1)
                if isinstance(b, int) and b == FULL:
                    sp.dma_start(x_in[0:REST, ring, :], x_rest).then_inc(x_loaded[ring], 16)
                else:
                    sp.dma_start(x_in[:, ring, :], x_blocks[b]).then_inc(x_loaded[ring], 16)

            def store_block(b, ring):
                rows = y[:, ring, :, :].rearrange("p c f -> p (c f)")
                wait(sp, result_ready, b + 1)
                if isinstance(b, int) and b == FULL:
                    sp.dma_start(out_rest, rows[0:REST]).then_inc(result_stored[ring], 16)
                else:
                    sp.dma_start(out_blocks[b], rows).then_inc(result_stored[ring], 16)

            for b in range(RING):
                load_block(b, b)
            way = take_way(sp)
            with sp.If(way == 1):
                def load_and_store(turn):
                    for r in range(RING):
                        load_block(turn * RING + r, r)
                        if not isinstance(turn, int) or turn > 1 or r >= RESULT_LAG:
                            store_block((turn - 1) * RING + r - RESULT_LAG, (r - RESULT_LAG) % RING)

                load_and_store(1)
                with sp.Fori(2, BLOCK_TURNS - 1) as turn:
                    load_and_store(turn)
                load_and_store(BLOCK_TURNS - 1)
                for b in range(BLOCKS - RING - RESULT_LAG, BLOCKS):
                    store_block(b, b % RING)
            with sp.If(way == 0):
                sp.wait_ge(dve_set, DVE_SETS)
                sp.dma_start(table_blocks.rearrange("b p n -> p b n"),
                             zero_rows.unsqueeze(1).to_broadcast([P, FULL, NPP * ROW])).then_inc(table_started, 16)
                sp.dma_start(table_rest, zero_rows[0:REST]).then_inc(table_started, 16)
                sp.wait_ge(table_done, 1)

                def last_block(b):
                    wait(sp, end_stored, b * 16)
                    rest = isinstance(b, int) and b == FULL
                    rows = REST if rest else P
                    sp.dma_start(end_sums[0:rows].rearrange("p c f -> p (c f)"),
                                 table_rest if rest else table_blocks[b]).then_inc(end_loaded, 16)
                    sp.dma_start(end_x[0:rows].rearrange("p c f -> p (c f)"),
                                 x_rest if rest else x_blocks[b]).then_inc(end_loaded, 16)
                    sp.wait_ge(end_ready, b + 1)
                    sp.dma_start(out_rest if rest else out_blocks[b],
                                 end_y[0:rows].rearrange("p c f -> p (c f)")).then_inc(end_stored, 16)

                last_block(0)
                with sp.Fori(1, FULL) as b:
                    last_block(b)
                last_block(FULL)
                sp.wait_ge(end_stored, 16 * BLOCKS)

        @block.scalar
        def _(act):
            act.wait_ge(zeros_set, 6)
            act.wait_ge(dve_set, 9)

            def column(v):
                return v.rearrange("(n a) -> n a", a=1)

            loads = []
            for h in (0, 1):
                loads += [(w1_pair[64 * h:64 * h + 64, 64 * h:64 * h + 64], W1),
                          (w2_twice[64 * h:64 * h + 64, :], W2),
                          (w4_pair[64 * h:64 * h + 64, D * h:D * h + D], W4),
                          (b1_sb[64 * h:64 * h + 64, :], column(b1)),
                          (b3_sb[64 * h:64 * h + 64, :], column(b3))]
                loads.append((w1_slot[64 * h:64 * h + D, 64 * h:64 * h + 64], W1[0:D, :]))
            for q in range(4):
                loads.append((w1_self[D * q:D * q + D, 64 * (q % 2):64 * (q % 2) + 64], W1[0:D, :]))
            loads += [(w3_sb[:, :], W3), (b2_sb[:, :], column(b2)),
                      (base_row[:, 0:D], b4.rearrange("(a n) -> a n", a=1).to_broadcast([P, D]))]
            assert len(loads) == WEIGHT_LOADS
            for place, what in loads:
                act.dma_start(place, what).then_inc(weights_in, 16)

            def end_root(c, number):
                act.wait_ge(end_summed, number + 1)
                act.activation(end_std[:, 0:c], end_mean[:, 0:c], ACT.Sqrt, bias=eps[:, 0:1],
                               scale=1.0 / D).then_inc(end_std_ready, 1)

            way = take_way(act)
            long_rows = take_long(act)
            with act.If(way == 1):
                act.wait_ge(weights_in, 16 * WEIGHT_LOADS)

                act.wait_ge(dve_set, DVE_SETS)

                def act_step(st):
                    u = st.of(EVERY) if st.has() else st.ref
                    if st.has():
                        if NORM_AT[st.ref] >= 0:
                            norm(st)
                        if st.kind() == "X" and st.ref >= X_AT[EARLY]:
                            if BATCH_OF[st.ref] >= 4:
                                slot_root(st.of(BATCH_OF) - 4)
                    if st.has(1) and st.kind(1) in "AX":
                        par = TILE_BUFFER[st.ref + 1]
                        act.wait_ge(transposed, st.of(TILE_OF, 1) + 1)
                        wait(act, h1_done, st.of(FREE_AT, 1))
                        act.activation(xT[:, par, :], t_ps[par][:, :], ACT.Copy).then_inc(xT_ready, 1)
                    if st.has():
                        act.wait_ge(h1_done, u + 1)
                        wait(act, h2_done, (u - 1) * 2)
                        act.activation(h1[:, st.ref % 2, :], h1_ps[:, :], ACT.Relu, bias=b1_sb[:, 0:1]).then_inc(h1_ready, 1)
                    if st.has(-1):
                        for j in range(2):
                            act.wait_ge(h2_done, (u - 1) * 2 + j + 1)
                            wait(act, h3_done, (u - 2) * 2)
                            act.activation(h2[:, (st.ref - 1) % 2, j, :], h2_ps[j][:, :], ACT.Relu,
                                           bias=b2_sb[:, 0:1]).then_inc(h2_ready, 1)
                    if st.has(-2):
                        act.wait_ge(h3_done, (u - 1) * 2)
                        wait(act, msg_done, u - 3)
                        act.activation(h3[:, st.ref % 2, :], h3_ps[:, :], ACT.Relu, bias=b3_sb[:, 0:1]).then_inc(h3_ready, 1)
                    if st.has(-3) and st.kind(-3) in "AB":
                        half = "AB".index(st.kind(-3))
                        act.wait_ge(msg_done, u - 2)
                        place = self_msg[:, st.place(BLOCK_OF, RING, -3), :].rearrange("p (k h n) -> p k h n", k=4, h=2)
                        act.activation(place[:, :, half, :], self_ps[:, 0:256].rearrange("p (k n) -> p k n", k=4),
                                       ACT.Copy).then_inc(self_stored, 1)

                def norm(st):
                    n, ref = st.of(NORM_AT), NORM_AT[st.ref]
                    if 0 <= ref - SQUARE_LAG < BLOCKS:
                        b, r = n - SQUARE_LAG, (ref - SQUARE_LAG) % RING
                        act.wait_ge(y_ready, b + 1)
                        wait(act, square_summed, b if r == 0 else b - 1)
                        act.activation(square[:, r % 2, :, :], y[:, r, :, :], ACT.Square).then_inc(square_ready, 1)
                    if 0 <= ref - ROOT_LAG < BLOCKS:
                        b, r = n - ROOT_LAG, (ref - ROOT_LAG) % RING
                        act.wait_ge(square_summed, b + 1)
                        act.activation(std[:, r, :], square_sum[:, r, :], ACT.Sqrt, bias=eps[:, 0:1],
                                       scale=1.0 / D).then_inc(std_ready, 1)

                def slot_root(batch):
                    act.wait_ge(slot_sums_ready, batch + 1)
                    act.activation(slot_std[:, bass.ds(batch * TOP, TOP)], slot_square_sum[:, bass.ds(batch * TOP, TOP)],
                                   ACT.Sqrt, bias=eps[:, 0:1], scale=1.0 / D).then_inc(slot_std_ready, 1)

                act.wait_ge(transposed, 1)
                act.activation(xT[:, 0, :], t_ps[0][:, :], ACT.Copy).then_inc(xT_ready, 1)
                run_steps(act, act_step)
                for long, last in ((1, len(UNITS)), (0, SHORT)):
                    with act.If(long_rows == long):
                        run_last_steps(act_step, last)
                        for batch in range(BATCHES - 6 + 2 * long, BATCHES - 2 + 2 * long):
                            slot_root(batch)
                end_root(1, 0)
            with act.If(way == 0):
                act.wait_ge(weights_in, 16 * WEIGHT_LOADS)
                def act_tile(t):
                    act.wait_ge(tile_pe, t * 7 + 1)
                    act.activation(xT[:, 0, 0:P], t_ps[0][:, 0:P], ACT.Copy).then_inc(tile_act, 1)
                    act.wait_ge(tile_pe, t * 7 + 2)
                    act.activation(h1[:, 0, 0:P], h1_ps[:, 0:P], ACT.Relu, bias=b1_sb[:, 0:1]).then_inc(tile_act, 1)
                    for j in range(2):
                        act.wait_ge(tile_pe, t * 7 + 3 + j)
                        act.activation(h2[:, 0, j, 0:P], h2_ps[j][:, 0:P], ACT.Relu, bias=b2_sb[:, 0:1]).then_inc(tile_act, 1)
                    act.wait_ge(tile_pe, t * 7 + 6)
                    act.activation(h3[:, 0, 0:P], h3_ps[:, 0:P], ACT.Relu, bias=b3_sb[:, 0:1]).then_inc(tile_act, 1)

                act_tile(0)
                with act.Fori(1, EDGE_COLS) as t:
                    act_tile(t)

                end_root(NPP, 0)
                with act.Fori(1, BLOCKS) as b:
                    end_root(NPP, b)

        @block.tensor
        def _(pe):
            pe.wait_ge(consts_set, 4)
            pe.wait_ge(stats_ready, 1)
            pe.matmul(extra_ps[:, 0:4], ones[:, :], stats[:, :], start=True, stop=True)
            pe.matmul(extra_ps[:, 4:5], before[:, :], extras_in_row[:, :], start=True, stop=True).then_inc(totals_ready, 1)

            def merge(number):
                pe.wait_ge(diag_ready, number)
                pe.matmul(t_ps[1][:, 0:P], ones[:, :], dst_diag[:, :], start=True, stop=True).then_inc(dst_spread, 1)
                pe.wait_ge(equal_ready, number)

            way = take_way(pe)
            long_rows = take_long(pe)
            with pe.If(way == 1):
                pe.wait_ge(weights_in, 16 * WEIGHT_LOADS)

                def transposes(st, shift):
                    par = TILE_BUFFER[st.ref + shift]
                    wait(pe, xT_ready, st.of(COPIED_AT, shift))
                    if st.kind(shift) == "X":
                        pe.wait_ge(pair_ready, st.of(BATCH_OF, shift) + 1)
                        buf = BUFFER_OF_BATCH[BATCH_OF[st.ref + shift]]
                        tile = x_pair[:, buf, :, :].rearrange("p s f -> p (s f)")
                    else:
                        ring = st.place(BLOCK_OF, RING, shift)
                        pe.wait_ge(x_loaded[ring], st.of(ROUND_OF, shift) * 16 + 16)
                        tile = x_in[:, ring, :]
                    for j in range(4):
                        last = pe.transpose(t_ps[par][:, j * P:(j + 1) * P], tile[:, j * P:(j + 1) * P], ident[:, :])
                    last.then_inc(transposed, 1)

                def pe_step(st):
                    u = st.of(EVERY) if st.has() else st.ref
                    if st.has(1) and st.kind(1) in "AX":
                        transposes(st, 1)
                    if st.has():
                        par = TILE_BUFFER[st.ref]
                        pe.wait_ge(xT_ready, st.of(TILE_OF) + 1)
                        wait(pe, h1_ready, u)
                        lo, hi, w = {"A": (0, 64, w1_self), "B": (64, P, w1_self), "X": (0, P, w1_pair),
                                     "S": (0, P, w1_slot)}[st.kind()]
                        pe.matmul(h1_ps[:, :], w[lo:hi, :], xT[lo:hi, par, :], start=True, stop=True).then_inc(h1_done, 1)
                    if st.has(-1):
                        pe.wait_ge(h1_ready, u)
                        for j in range(2):
                            wait(pe, h2_ready, (u - 2) * 2 + j + 1)
                            pe.matmul(h2_ps[j][:, :], w2_twice[64 * j:64 * j + 64, :],
                                      h1[64 * j:64 * j + 64, (st.ref - 1) % 2, :], start=True, stop=True).then_inc(h2_done, 1)
                    if st.has(-2):
                        wait(pe, h3_ready, u - 2)
                        for j in range(2):
                            pe.wait_ge(h2_ready, (u - 2) * 2 + j + 1)
                            pe.matmul(h3_ps[64 * j:64 * j + 64, :], w3_sb[:, :], h2[:, st.ref % 2, j, :],
                                      start=True, stop=True).then_inc(h3_done, 1)
                    if st.has(-3):
                        k = st.kind(-3)
                        pe.wait_ge(h3_ready, u - 2)
                        if k == "X":
                            wait(pe, extras_taken, st.of(BATCH_OF, -3))
                        elif k in "AB":
                            wait(pe, self_stored, st.of(BLOCK_OF, -3) * 2 + "AB".index(k))
                        place = self_ps if k in "AB" else extra_ps[:, "XS".index(k) * 256:]
                        for j in range(4):
                            last = pe.matmul(place[:, 64 * j:64 * j + 64], h3[:, (st.ref - 3) % 2, j * P:(j + 1) * P],
                                             w4_pair[:, :], start=True, stop=True)
                        last.then_inc(msg_done, 1)

                transposes(Step(0), 0)
                run_steps(pe, pe_step)
                for long, last in ((1, len(UNITS)), (0, SHORT)):
                    with pe.If(long_rows == long):
                        run_last_steps(pe_step, last)
                merge(1)
                pe.matmul(self_ps[:, 0:ROW], equal[:, :], part_sum[:, 0, :], start=True, stop=False)
                pe.matmul(self_ps[:, 0:ROW], equal_last[:, :], part_sum[:, 1, :], start=False, stop=True).then_inc(merged, 1)

            with pe.If(way == 0):
                pe.wait_ge(weights_in, 16 * WEIGHT_LOADS)
                def pe_tile(t):
                    pe.wait_ge(tile_diff, t + 1)
                    pe.transpose(t_ps[0][:, 0:P], tile_x[:, :], ident[:, :]).then_inc(tile_pe, 1)
                    pe.wait_ge(tile_act, t * 5 + 1)
                    pe.matmul(h1_ps[:, 0:P], w1_pair[:, :], xT[:, 0, 0:P], start=True, stop=True).then_inc(tile_pe, 1)
                    pe.wait_ge(tile_act, t * 5 + 2)
                    for j in range(2):
                        pe.matmul(h2_ps[j][:, 0:P], w2_twice[64 * j:64 * j + 64, :], h1[64 * j:64 * j + 64, 0, 0:P],
                                  start=True, stop=True).then_inc(tile_pe, 1)
                    for j in range(2):
                        pe.wait_ge(tile_act, t * 5 + 3 + j)
                        pe.matmul(h3_ps[64 * j:64 * j + 64, 0:P], w3_sb[:, :], h2[:, 0, j, 0:P],
                                  start=True, stop=True).then_inc(tile_pe, 1)
                    pe.wait_ge(tile_act, t * 5 + 5)
                    pe.matmul(extra_ps[:, 0:64], h3[:, 0, 0:P], w4_pair[:, :], start=True, stop=True).then_inc(tile_pe, 1)
                    merge(t + 1)
                    pe.wait_ge(tile_msg_ready, t + 1)
                    pe.matmul(self_ps[:, 0:ROW], equal[:, :], tile_msg[:, :], start=True, stop=True).then_inc(merged, 1)

                pe_tile(0)
                with pe.Fori(1, EDGE_COLS) as t:
                    pe_tile(t)

        @block.gpsimd
        def _(pool):
            steps = Count(pool, pool_steps)
            pool.memset(w1_pair[:, :], 0.0).then_inc(zeros_set, 1)
            pool.memset(w1_self[:, :], 0.0).then_inc(zeros_set, 1)
            pool.memset(w4_pair[:, :], 0.0).then_inc(zeros_set, 1)
            pool.memset(w1_slot[:, :], 0.0).then_inc(zeros_set, 1)
            pool.memset(base_row[:, :], 1.0).then_inc(zeros_set, 1)
            pool.iota(countdown, [[-1, EDGE_COLS]], base=KEY_TOP, channel_multiplier=0).then_inc(consts_set, 1)
            pool.iota(row_start[:, :], [[0, 1]], base=KEY_TOP, channel_multiplier=EDGE_COLS,
                      allow_small_or_imprecise_dtypes=True).then_inc(zeros_set, 1)
            pool.iota(minus_slot[:, :], [[-1, SLOTS]], base=0, channel_multiplier=0,
                      allow_small_or_imprecise_dtypes=True).then_inc(consts_set, 1)
            steps.up(pool.memset(ident[:, :], 0.0))
            steps.up(pool.memset(ones[:, :], 1.0))
            steps.settle()
            pool.affine_select(out=ident[:, :], in_=ident[:, :], compare_op=ALU.not_equal, fill=1.0, base=0,
                               pattern=[[-1, P]], channel_multiplier=1).then_inc(consts_set, 1)
            steps.up(pool.affine_select(out=before[:, :], in_=ones[:, :], compare_op=ALU.is_gt, fill=0.0, base=0,
                                        pattern=[[1, P]], channel_multiplier=-1))
            steps.up(pool.affine_select(out=earlier[:, :], in_=ones[:, :], compare_op=ALU.is_gt, fill=0.0, base=0,
                                        pattern=[[-1, P]], channel_multiplier=1))
            steps.settle()
            pool.drain().then_inc(consts_set, 1)

            marks = Count(pool, pool_marks)

            def hold(semaphore, value):
                if isinstance(value, int) and value <= 0:
                    return
                pool.wait_ge(semaphore, value)
                marks.settle()
                marks.up(pool.tensor_tensor(pool_mark[:, :], ones[:, 0:1], ones[:, 0:1], ALU.add))

            def merge_gather(number):
                hold(merge_asked, number)
                pool.indirect_dma_start(table_rows[:, :], None, table[:, :],
                                        bass.IndirectOffsetOnAxis(merge_index[:, 0:1], 0)).then_inc(merge_gathered, 16)

            def merge_scatter(number):
                hold(merge_rows_ready, number)
                pool.indirect_dma_start(table[:, :], bass.IndirectOffsetOnAxis(merge_out[:, 0:1], 0), new_rows[:, :], None,
                                        bounds_check=N - 1, oob_is_err=False).then_inc(merge_stored, 16)

            marks_before = marks.n
            way = take_way(pool)
            long_rows = take_long(pool)
            with pool.If(way == 1):
                def gather(turn, i):
                    batch = turn * LANDINGS + i
                    hold(batch_kept, (batch - LANDINGS + 1) * 2)
                    pool.wait_ge(slots_found, batch + 1)
                    marks.settle()
                    marks.up(pool.tensor_copy(ends_now[:, i, :, :],
                                              ends_index[:, bass.ds(batch, 1), :, :].rearrange("p b k s -> p (b k) s")))
                    hold(pool_marks, marks.n)
                    for s in range(TOP):
                        for k in range(2):
                            pool.indirect_dma_start(
                                gathered[:, i, s, k * D:(k + 1) * D], None, x[:, :],
                                bass.IndirectOffsetOnAxis(ends_now[:, i, k, s:s + 1], 0)
                            ).then_inc(batch_gathered[i], 16)

                def scatter(turn, i):
                    hold(rows_ready, (turn * 2 + i) * 2 + 2)
                    for s in range(TOP):
                        pool.indirect_dma_start(
                            out[:, :], bass.IndirectOffsetOnAxis(out_now[:, i, s:s + 1], 0), rows_now[:, i, s, :], None,
                            bounds_check=N - 1, oob_is_err=False).then_inc(rows_stored[i], 16)

                for i in range(LANDINGS):
                    gather(0, i)
                start, built = marks.n, marks.built
                with pool.Fori(1, BATCHES // LANDINGS) as turn:
                    marks.n = (turn - 1) * (LANDINGS * 3) + start
                    for i in range(LANDINGS):
                        gather(turn, i)
                assert marks.built == built + LANDINGS * 3
                marks.n = start + (BATCHES // LANDINGS - 1) * LANDINGS * 3
                with pool.If(long_rows == 1):
                    for i in range(BATCHES % LANDINGS):
                        gather(BATCHES // LANDINGS, i)
                marks.n = start + (BATCHES // LANDINGS - 1) * LANDINGS * 3
                with pool.If(long_rows == 0):
                    for _ in range(BATCHES % LANDINGS * 3):
                        hold(slots_found, 1)
                for ring in range(RING):
                    hold(result_stored[ring], 16 * BLOCK_TURNS)
                scatter(0, 0)
                scatter(0, 1)
                start, built = marks.n, marks.built
                with pool.Fori(1, BATCHES // 2 - 1) as turn:
                    marks.n = (turn - 1) * 2 + start
                    scatter(turn, 0)
                    scatter(turn, 1)
                assert marks.built == built + 2
                before_last = start + (BATCHES // 2 - 2) * 2
                marks.n = before_last
                with pool.If(long_rows == 1):
                    scatter(BATCHES // 2 - 1, 0)
                    scatter(BATCHES // 2 - 1, 1)
                    for i in range(2):
                        hold(rows_stored[i], 16 * SLOTS // 2)
                marks.n = before_last
                with pool.If(long_rows == 0):
                    for i in range(2):
                        hold(rows_ready, 2 * (BATCHES - 2))
                        hold(rows_stored[i], 16 * (SLOTS // 2 - TOP))
                hold(end_ready, 1)
                pool.indirect_dma_start(out[:, :], bass.IndirectOffsetOnAxis(merge_out[:, 0:1], 0), end_row[:, :], None,
                                        bounds_check=N - 1, oob_is_err=False).then_inc(merge_stored, 16)
                hold(merge_stored, 16)
            with pool.If(way == 0):
                marks.n = marks_before
                hold(table_started, 32)

                def pool_tile(t):
                    hold(merge_asked, t + 1)
                    pool.indirect_dma_start(tile_x[:, 0:D], None, x[:, :],
                                            bass.IndirectOffsetOnAxis(merge_index[:, 0:1], 0)).then_inc(tile_gathered, 16)
                    pool.indirect_dma_start(tile_x[:, D:2 * D], None, x[:, :],
                                            bass.IndirectOffsetOnAxis(merge_src[:, 0:1], 0)).then_inc(tile_gathered, 16)
                    hold(merge_stored, t * 16)
                    merge_gather(t + 1)
                    merge_scatter(t + 1)

                pool_tile(0)
                start, built = marks.n, marks.built
                with pool.Fori(1, EDGE_COLS) as t:
                    marks.n = (t - 1) * TILE_MARKS + start
                    pool_tile(t)
                assert marks.built == built + TILE_MARKS
                marks.n = start + (EDGE_COLS - 1) * TILE_MARKS
                hold(merge_stored, 16 * EDGE_COLS)
                pool.drain().then_inc(table_done, 1)

        @block.vector
        def _(dve):
            steps = Count(dve, dve_steps)

            def merge_start(column, number):
                dve.tensor_scalar(merge_index[:, :], column, float(N - 1), None, ALU.min).then_inc(merge_asked, 1)
                dve.tensor_scalar(dst_diag[:, :], ident[:, :], column, None, ALU.mult).then_inc(diag_ready, 1)

            def merge_equal(column, number):
                dve.wait_ge(dst_spread, number)
                dve.tensor_scalar(equal[:, :], t_ps[1][:, 0:P], column, None, ALU.is_equal).then_inc(equal_ready, 1)
                dve.wait_ge(equal_ready, number)
                steps.up(dve.tensor_tensor_reduce(equal_earlier[:, :], equal[:, :], earlier[:, :], 1.0, 0.0,
                                                  ALU.mult, ALU.add, repeats[:, :]))
                steps.settle()
                steps.up(dve.tensor_scalar(first_of[:, :], repeats[:, :], 0.0, None, ALU.is_equal))
                steps.up(dve.tensor_scalar(shifted[:, :], column, float(NOWHERE), None, ALU.subtract))
                steps.settle()
                steps.up(dve.tensor_tensor(first_of[:, :], first_of[:, :], shifted[:, :], ALU.mult))
                steps.settle()
                steps.up(dve.tensor_scalar(merge_out[:, :], first_of[:, :], float(NOWHERE), None, ALU.add))

            def merge_finish(totals, number):
                dve.wait_ge(merged, number)
                dve.wait_ge(merge_gathered, number * 16)
                steps.settle()
                dve.tensor_tensor(new_rows[:, :], table_rows[:, :], totals, ALU.add).then_inc(merge_rows_ready, 1)

            dve.memset(dst_sb[96:P, LAST_COLS:EDGE_COLS], NOWHERE).then_inc(pads_set, 1)
            dve.memset(nxt_sb[96:P, LAST_COLS - 1:EDGE_COLS], NOWHERE).then_inc(pads_set, 1)
            dve.memset(src_sb[96:P, LAST_COLS:EDGE_COLS], 0).then_inc(pads_set, 1)
            dve.memset(msg[:, :, :], 1.0).then_inc(dve_set, 1)
            dve.memset(same_run[:, :, :], 0.0).then_inc(dve_set, 1)
            dve.memset(run_sum[:, :, :], 0.0).then_inc(dve_set, 1)
            dve.memset(part_sum[:, :, :], 0.0).then_inc(dve_set, 1)
            dve.memset(tile_msg[:, :], 1.0).then_inc(dve_set, 1)
            dve.memset(eps[:, :], EPS).then_inc(dve_set, 1)
            dve.memset(zero_rows, 0.0).then_inc(dve_set, 1)
            dve.memset(tile_x[:, 2 * D:4 * D], 0.0).then_inc(dve_set, 1)
            dve.memset(dst_of_slot[:, 0:1], -1.0).then_inc(dve_set, 1)
            dve.memset(dst_of_slot[:, SLOTS + 1:SLOTS + 2], float(NOWHERE)).then_inc(dve_set, 1)
            dve.wait_ge(edges_in, 16 * EDGE_LOADS)
            steps.up(dve.tensor_tensor(work_a, src_sb[:, :], dst_sb[:, :], ALU.is_equal))
            steps.up(dve.tensor_tensor(work_b, nxt_sb[:, :], dst_sb[:, :], ALU.not_equal))
            steps.settle()
            steps.up(dve.tensor_tensor_reduce(work_a, work_a, work_b, 1.0, 0.0,
                                              ALU.mult, ALU.add, stats[:, 0:1]))
            steps.settle()
            steps.up(dve.tensor_tensor_reduce(work_b, dst_sb[:, :], nxt_sb[:, :], 1.0, 0.0,
                                              ALU.subtract, ALU.max, largest_fall[:, :]))
            steps.up(dve.scalar_tensor_tensor(out=extra, in0=dst_sb[:, :], scalar=float(NOWHERE), in1=work_a,
                                              op0=ALU.is_lt, op1=ALU.subtract, accum_out=extras_in_row[:, :]))
            steps.settle()
            steps.up(dve.tensor_scalar(stats[:, 1:2], largest_fall[:, :], 0.0, None, ALU.is_gt))
            steps.up(dve.tensor_scalar(stats[:, 2:3], extras_in_row[:, :], float(SLOTS), None, ALU.is_gt))
            steps.up(dve.tensor_scalar(stats[:, 3:4], extras_in_row[:, :], float(SLOTS - 2 * TOP), None, ALU.is_gt))
            steps.settle()
            dve.drain().then_inc(stats_ready, 1)
            steps.up(dve.tensor_tensor(work_b, dst_sb[:, :], extra, ALU.mult))
            steps.settle()
            steps.up(dve.tensor_reduce(last_dst[:, :], work_b, AX.X, ALU.max))
            dve.wait_ge(consts_set, 4)
            steps.up(dve.tensor_tensor(key[:, :], extra, countdown, ALU.mult))
            steps.up(dve.tensor_tensor(nxt_sb[:, :], extra, src_sb[:, :], ALU.mult))
            steps.settle()
            steps.up(dve.tensor_scalar(key[:, :], key[:, :], SRC_BITS, None, ALU.logical_shift_left))
            steps.settle()
            steps.up(dve.tensor_tensor(key[:, :], key[:, :], nxt_sb[:, :], ALU.bitwise_or))
            dve.wait_ge(totals_ready, 1)
            dve.wait_ge(zeros_set, 6)
            steps.up(dve.tensor_scalar(checks[:, 0:1], extra_ps[:, 0:1], float(N), None, ALU.is_equal))
            steps.up(dve.tensor_scalar(checks[:, 1:3], extra_ps[:, 1:3], 0.0, None, ALU.is_equal))
            steps.up(dve.tensor_scalar(long_f[:, :], extra_ps[:, 3:4], 0.0, None, ALU.is_gt))
            steps.up(dve.tensor_tensor(node_base[:, :], row_start[:, :], extra_ps[:, 4:5], ALU.subtract))
            steps.settle()
            steps.up(dve.tensor_tensor(flag_f[:, :], checks[:, 0:1], checks[:, 1:2], ALU.mult))
            steps.settle()
            steps.up(dve.tensor_tensor(flag_f[:, :], flag_f[:, :], checks[:, 2:3], ALU.mult))
            steps.up(dve.tensor_scalar(slot_base[:, :], minus_slot[:, :], node_base[:, 0:1], None, ALU.add))
            steps.settle()
            dve.tensor_copy(flag[:, :], flag_f[:, :]).then_inc(flag_ready, 1)
            dve.tensor_copy(long_flag[:, :], long_f[:, :]).then_inc(flag_ready, 1)
            dve.wait_ge(weights_in, 16 * WEIGHT_LOADS)
            dve.wait_ge(dve_set, DVE_SETS)

            def of_batch(slots, batch):
                return slots[:, bass.ds(batch, 1), :].rearrange("p b s -> p (b s)")

            def search(batch):
                steps.settle()
                steps.up(dve.memset(mark[:, :], 0.0))
                steps.up(dve.max(out=top[:, :], in_=key_f))
                steps.settle()
                steps.up(dve.memset(mark[:, :], 0.0))
                steps.up(dve.match_replace(out=key_f, in_to_replace=top[:, :], in_values=key_f, imm_value=0.0))
                slots = bass.ds(batch * TOP, TOP)
                steps.up(dve.tensor_scalar(of_batch(ends_index[:, :, 1, :], batch), top_bits, (1 << SRC_BITS) - 1, None, ALU.bitwise_and))
                steps.up(dve.tensor_scalar(key_count[:, :], top_bits, SRC_BITS, None, ALU.logical_shift_right))
                steps.settle()
                steps.up(dve.tensor_scalar(found[:, :], key_count[:, :], 0.0, None, ALU.is_gt))
                steps.up(dve.tensor_tensor(slot_dst[:, :], slot_base[:, slots], key_count[:, :], ALU.subtract))
                steps.settle()
                steps.up(dve.tensor_tensor(of_batch(ends_index[:, :, 0, :], batch), slot_dst[:, :], found[:, :], ALU.mult))
                steps.up(dve.scalar_tensor_tensor(out=slot_dst[:, :], in0=slot_dst[:, :], scalar=float(NOWHERE),
                                                  in1=found[:, :], op0=ALU.subtract, op1=ALU.mult))
                steps.settle()
                dve.tensor_scalar(dst_of_slot[:, bass.ds(batch * TOP + 1, TOP)], slot_dst[:, :],
                                  float(NOWHERE), None, ALU.add).then_inc(slots_found, 1)

            def keep(batch, i):
                dve.wait_ge(batch_gathered[i], (batch - i) * (16 * 2 * TOP // LANDINGS) + 16 * 2 * TOP)
                here = kept[:, bass.ds(batch, 1), :, :].rearrange("p b s f -> p (b s) f")
                dve.tensor_copy(here[:, :, 0:D], gathered[:, i, :, 0:D]).then_inc(batch_kept, 1)
                dve.tensor_tensor(here[:, :, D:2 * D], gathered[:, i, :, D:2 * D], gathered[:, i, :, 0:D],
                                  ALU.subtract).then_inc(batch_kept, 1)

            def stage(batch, ref):
                buf = BUFFER_OF_BATCH[ref]
                last = max([b for b in range(ref) if BUFFER_OF_BATCH[b] == buf], default=None)
                if last is not None:
                    wait(dve, transposed, moved(batch, ref, TILE_OF_BATCH, TILE_OF_BATCH[last] + 1))
                dve.wait_ge(batch_kept, batch * 2 + 2)
                dve.tensor_copy(x_pair[:, buf, :, :].rearrange("p s f -> p (s f)"),
                                kept[:, bass.ds(batch, 1), :, :].rearrange("p b s f -> p (b s f)")).then_inc(pair_ready, 1)

            def moved(batch, ref, numbers, value):
                if isinstance(batch, int):
                    return value
                per_batch = numbers[ref] - numbers[ref - 1]
                return batch * per_batch + (value - ref * per_batch)

            def look_at_runs():
                here, left, right = dst_of_slot[:, 1:SLOTS + 1], dst_of_slot[:, 0:SLOTS], dst_of_slot[:, 2:SLOTS + 2]
                first = dst_of_slot[:, 1:2]
                dve.wait_ge(slots_found, BATCHES)
                steps.up(dve.tensor_tensor(same_run[:, :, 1:TOP + 1], here.rearrange("p (b s) -> p b s", s=TOP),
                                           left.rearrange("p (b s) -> p b s", s=TOP), ALU.is_equal))
                steps.up(dve.tensor_scalar(part_mask[:, 0, :], here, first, None, ALU.is_equal))
                steps.up(dve.tensor_scalar(not_first[:, :], here, first, None, ALU.not_equal))
                steps.up(dve.tensor_scalar(part_mask[:, 1, :], here, last_dst[:, 0:1], None, ALU.is_equal))
                steps.up(dve.tensor_tensor(run_end[:, :], here, right, ALU.not_equal))
                steps.settle()
                steps.up(dve.tensor_tensor(part_mask[:, 1, :], part_mask[:, 1, :], not_first[:, :], ALU.mult))
                steps.up(dve.tensor_tensor(run_end[:, :], run_end[:, :], not_first[:, :], ALU.mult))
                steps.settle()
                steps.up(dve.scalar_tensor_tensor(out=run_end[:, :], in0=here, scalar=float(NOWHERE), in1=run_end[:, :],
                                                  op0=ALU.subtract, op1=ALU.mult))
                steps.settle()
                steps.up(dve.tensor_scalar(out_index[:, :], run_end[:, :], float(NOWHERE), None, ALU.add))
                steps.settle()

            def runs(batch, ref, ahead=None, done=None, i=None, times=None):
                steps.settle()
                steps.up(dve.tensor_copy(msg[:, :, 0:1], run_sum[:, :, TOP:TOP + 1]))
                steps.up(dve.tensor_copy(go_on[:, :, :], same_run[:, bass.ds(batch, 1), :].to_broadcast([P, ROW, TOP + 1])))
                dve.wait_ge(msg_done, moved(batch, ref, X_AT, X_AT[ref] + 2))
                steps.up(dve.tensor_tensor(msg[:, 0:D, 1:TOP + 1], extra_ps[:, 0:TOP * D].rearrange("p (s f) -> p f s", f=D),
                                           base_row[:, 0:D].unsqueeze(2).to_broadcast([P, D, TOP]), ALU.add))
                messages = steps.n
                dve.tensor_tensor(slot_msg[:, :, :], extra_ps[:, TOP * D:2 * TOP * D].rearrange("p (s f) -> p s f", f=D),
                                  base_row[:, 0:D].unsqueeze(1).to_broadcast([P, TOP, D]), ALU.add).then_inc(extras_taken, 1)
                if isinstance(batch, int) and batch == 0:
                    dve.wait_ge(extras_taken, 1)
                    steps.up(dve.tensor_copy(first_self[:, :], slot_msg[:, 0, :]))
                    steps.up(dve.tensor_copy(first_x[:, :], kept[:, 0, 0, 0:D]))
                steps.settle(messages)
                steps.up(dve.tensor_tensor_scan(run_sum[:, :, :].rearrange("p f s -> p (f s)"),
                                                go_on[:, :, :].rearrange("p f s -> p (f s)"),
                                                msg[:, :, :].rearrange("p f s -> p (f s)"), 0.0, ALU.mult, ALU.add))
                sums = steps.n
                steps.up(dve.tensor_tensor(part[:, :, :, :], msg[:, :, 1:TOP + 1].unsqueeze(1).to_broadcast([P, 2, ROW, TOP]),
                                           part_mask[:, :, bass.ds(batch * TOP, TOP)].unsqueeze(2).to_broadcast(
                                               [P, 2, ROW, TOP]), ALU.mult))
                parts = steps.n
                steps.settle(sums)
                steps.up(dve.tensor_scalar(slot_count[:, :], run_sum[:, D, 1:TOP + 1], 1.0, None, ALU.add))
                counts = steps.n
                dve.wait_ge(extras_taken, batch + 1)
                steps.up(dve.tensor_tensor(slot_msg[:, :, :], slot_msg[:, :, :],
                                           run_sum[:, 0:D, 1:TOP + 1].rearrange("p f s -> p s f"), ALU.add))
                steps.settle(counts)
                steps.up(dve.reciprocal(slot_share[:, :], slot_count[:, :]))
                shares = steps.n
                steps.settle(parts)
                steps.up(dve.tensor_reduce(part_add[:, :, :], part[:, :, :, :], AX.X, ALU.add))
                additions = steps.n
                steps.settle(shares)
                steps.up(dve.tensor_tensor(slot_msg[:, :, :], slot_msg[:, :, :],
                                           slot_share[:, :].unsqueeze(2).to_broadcast([P, TOP, D]), ALU.mult))
                means = steps.n
                steps.settle(additions)
                steps.up(dve.tensor_tensor(part_sum[:, :, :], part_sum[:, :, :], part_add[:, :, :], ALU.add))
                steps.settle(means)
                steps.up(dve.tensor_tensor(slot_x[:, :, :], slot_msg[:, :, :], x_i_of(batch), ALU.add))
                slot_ys = steps.n
                if done is not None:
                    deviations(done)
                    deviated = steps.n
                steps.settle(slot_ys)
                steps.up(dve.tensor_reduce(slot_sum[:, :], slot_x[:, :, :], AX.X, ALU.add))
                slot_sums = steps.n
                if done is not None:
                    end_nodes(done, i, times)
                steps.settle(slot_sums)
                steps.up(dve.tensor_scalar(slot_mean[:, :], slot_sum[:, :], 1.0 / D, None, ALU.mult))
                slot_means = steps.n
                if done is not None:
                    results(done, i, deviated)
                steps.settle(slot_means)
                rows = x_i_of(batch)
                steps.up(dve.tensor_tensor(rows, slot_x[:, :, :],
                                           slot_mean[:, :].unsqueeze(2).to_broadcast([P, TOP, D]), ALU.subtract))
                centred = steps.n
                if ahead is not None:
                    stage(*ahead)
                steps.settle(centred)
                wait(dve, slot_sums_ready, batch)
                steps.up(dve.tensor_tensor(slot_square[:, :, :], rows, rows, ALU.mult))
                steps.settle()
                dve.tensor_reduce(slot_square_sum[:, bass.ds(batch * TOP, TOP)], slot_square[:, :, :], AX.X,
                                  ALU.add).then_inc(slot_sums_ready, 1)

            def x_i_of(batch):
                return kept[:, bass.ds(batch, 1), :, 0:D].rearrange("p b s f -> p (b s) f")

            def deviations(batch):
                dve.wait_ge(slot_std_ready, batch + 1)
                wait(dve, rows_ready, batch * 2)
                steps.up(dve.reciprocal(slot_rstd[:, :], slot_std[:, bass.ds(batch * TOP, TOP)]))

            def end_nodes(batch, i, times):
                wait(dve, rows_stored[i], times)
                dve.tensor_copy(out_now[:, i, :], out_index[:, bass.ds(batch * TOP, TOP)]).then_inc(rows_ready, 1)

            def results(batch, i, deviated):
                steps.settle(deviated)
                dve.tensor_tensor(rows_now[:, i, :, :], x_i_of(batch),
                                  slot_rstd[:, :].unsqueeze(2).to_broadcast([P, TOP, D]), ALU.mult).then_inc(rows_ready, 1)

            def finish(batch, i, times):
                deviations(batch)
                end_nodes(batch, i, times)
                results(batch, i, steps.n)

            def block(b, ref, round_):
                steps.settle()
                if ref < BLOCKS:
                    r = ref % RING
                    dve.wait_ge(self_stored, b * 2 + 2)
                    wait(dve, result_stored[r], round_ * 16)
                    dve.tensor_tensor(y[:, r, :, :], x_in[:, r, :].rearrange("p (c f) -> p c f", f=D),
                                      base_row[:, 0:D].unsqueeze(1).to_broadcast([P, NPP, D]), ALU.add).then_inc(y_begun, 1)
                    dve.wait_ge(y_begun, b + 1)
                    steps.up(dve.tensor_tensor(y[:, r, :, :], y[:, r, :, :],
                                               self_msg[:, r, :].rearrange("p (c f) -> p c f", f=D), ALU.add))
                    steps.settle()
                    steps.up(dve.tensor_reduce(y_sum[:, :], y[:, r, :, :], AX.X, ALU.add))
                    steps.settle()
                    steps.up(dve.tensor_scalar(y_mean[:, :], y_sum[:, :], 1.0 / D, None, ALU.mult))
                    steps.settle()
                    dve.tensor_tensor(y[:, r, :, :], y[:, r, :, :], y_mean[:, :].unsqueeze(2).to_broadcast([P, NPP, D]),
                                      ALU.subtract).then_inc(y_ready, 1)
                if 0 <= ref - SUM_LAG < BLOCKS:
                    c, r = b - SUM_LAG, (ref - SUM_LAG) % RING
                    dve.wait_ge(square_ready, c + 1)
                    dve.tensor_reduce(square_sum[:, r, :], square[:, r % 2, :, :], AX.X, ALU.add).then_inc(square_summed, 1)
                if 0 <= ref - RESULT_LAG < BLOCKS:
                    c, r = b - RESULT_LAG, (ref - RESULT_LAG) % RING
                    dve.wait_ge(std_ready, c + 1)
                    wait(dve, result_ready, c)
                    steps.up(dve.reciprocal(rstd[:, :], std[:, r, :]))
                    steps.settle()
                    dve.tensor_tensor(y[:, r, :, :], y[:, r, :, :], rstd[:, :].unsqueeze(2).to_broadcast([P, NPP, D]),
                                      ALU.mult).then_inc(result_ready, 1)
                if ref < BLOCKS:
                    dve.wait_ge(y_ready, b + 1)
                    steps.up(dve.memset(mark[:, :], 0.0))

            def end_layernorm(c, number):
                ys = end_y[:, 0:c, :]
                steps.settle()
                steps.up(dve.tensor_reduce(end_mean[:, 0:c], ys, AX.X, ALU.add))
                steps.settle()
                steps.up(dve.tensor_scalar(end_count[:, 0:c], end_mean[:, 0:c], 1.0 / D, None, ALU.mult))
                steps.settle()
                steps.up(dve.tensor_tensor(ys, ys, end_count[:, 0:c].unsqueeze(2).to_broadcast([P, c, D]), ALU.subtract))
                steps.settle()
                steps.up(dve.tensor_tensor(end_square[:, 0:c, :], ys, ys, ALU.mult))
                steps.settle()
                dve.tensor_reduce(end_mean[:, 0:c], end_square[:, 0:c, :], AX.X, ALU.add).then_inc(end_summed, 1)
                dve.wait_ge(end_std_ready, number + 1)
                steps.up(dve.reciprocal(end_count[:, 0:c], end_std[:, 0:c]))
                steps.settle()

            way = take_way(dve)
            long_rows = take_long(dve)
            with dve.If(way == 1):
                FIRST_SEARCHES, PER_TURN = 6, 4
                TURN_STEPS = RING * BLOCK_STEPS + PER_TURN * SEARCH_STEPS
                for batch in range(FIRST_SEARCHES):
                    search(batch)

                def turn_of_blocks(turn):
                    inside = not isinstance(turn, int)
                    for r in range(RING):
                        block(turn * RING + r, (RING if inside else turn * RING) + r, turn)
                        if r % 2 == 0 and (inside or turn > 0 or r >= 4):
                            keep(turn * LANDINGS + (r // 2 - 2), (r // 2 - 2) % LANDINGS)
                        if r < PER_TURN and (inside or turn < PLAIN_TURNS):
                            search(turn * PER_TURN + FIRST_SEARCHES + r)
                        if not inside and turn >= PLAIN_TURNS:
                            if r == 1:
                                stage(turn - PLAIN_TURNS, turn - PLAIN_TURNS)
                            if r == 3 and turn > PLAIN_TURNS:
                                runs(turn - PLAIN_TURNS - 1, turn - PLAIN_TURNS - 1)
                            if r in (3, 5) and turn == BLOCK_TURNS - 1:
                                stage(EARLY + (r - 3) // 2, EARLY + (r - 3) // 2)

                turn_of_blocks(0)
                start, built = steps.n, steps.built
                with dve.Fori(1, PLAIN_TURNS) as turn:
                    steps.n = (turn - 1) * TURN_STEPS + start
                    turn_of_blocks(turn)
                assert steps.built == built + TURN_STEPS, steps.built - built
                steps.n = start + (PLAIN_TURNS - 1) * TURN_STEPS
                assert FIRST_SEARCHES + PLAIN_TURNS * PER_TURN == BATCHES
                look_at_runs()
                for turn in range(PLAIN_TURNS, BLOCK_TURNS):
                    turn_of_blocks(turn)
                stage(EARLY + 2, EARLY + 2)
                block(BLOCKS, BLOCKS, 0)
                runs(EARLY - 1, EARLY - 1)
                block(BLOCKS + 1, BLOCKS + 1, 0)
                stage(EARLY + 3, EARLY + 3)
                block(BLOCKS + 2, BLOCKS + 2, 0)
                runs(EARLY, EARLY, ahead=(EARLY + 4, EARLY + 4))
                block(BLOCKS + 3, BLOCKS + 3, 0)
                for batch in (BATCHES - 4, BATCHES - 3):
                    keep(batch, batch % LANDINGS)
                with dve.If(long_rows == 1):
                    for batch in (BATCHES - 2, BATCHES - 1):
                        keep(batch, batch % LANDINGS)
                with dve.If(long_rows == 0):
                    dve.wait_ge(batch_kept, 2 * (BATCHES - 2))
                    for batch in (BATCHES - 2, BATCHES - 1):
                        for k in range(2):
                            dve.tensor_copy(kept[:, batch, :, k * D:(k + 1) * D],
                                            kept[:, batch - 2, :, k * D:(k + 1) * D]).then_inc(batch_kept, 1)

                def one_pair(pair):
                    for i in range(2):
                        batch, ref = pair * 2 + i, (pair if isinstance(pair, int) else 2) * 2 + i
                        ahead = (batch + 4, ref + 4) if not isinstance(pair, int) or batch + 4 < BATCHES else None
                        runs(batch, ref, ahead, done=pair * 2 + (i - 2), i=i, times=(pair - 1) * (16 * TOP))

                assert EARLY == 1
                one_pair(1)
                start, built = steps.n, steps.built
                with dve.Fori(2, BATCHES // 2 - 2) as pair:
                    steps.n = (pair - 2) * (2 * (RUNS_STEPS + FINISH_STEPS)) + start
                    one_pair(pair)
                assert steps.built == built + 2 * (RUNS_STEPS + FINISH_STEPS)
                steps.n = start + (BATCHES // 2 - 4) * 2 * (RUNS_STEPS + FINISH_STEPS)
                one_pair(BATCHES // 2 - 2)
                before_last = steps.n
                with dve.If(long_rows == 1):
                    one_pair(BATCHES // 2 - 1)
                    for i in range(2):
                        finish(BATCHES - 2 + i, i, (BATCHES // 2 - 1) * (16 * TOP))
                    steps.settle()
                steps.n = before_last
                with dve.If(long_rows == 0):
                    for i in range(2):
                        finish(BATCHES - 4 + i, i, (BATCHES // 2 - 2) * (16 * TOP))
                    steps.settle()
                steps = Count(dve, dve_end_steps)
                steps.settle()
                merge_start(dst_of_slot[:, 1:2], 1)
                dve.wait_ge(dst_spread, 1)
                steps.up(dve.tensor_scalar(equal_last[:, :], t_ps[1][:, 0:P], last_dst[:, 0:1], None, ALU.is_equal))
                steps.settle()
                merge_equal(dst_of_slot[:, 1:2], 1)
                dve.wait_ge(merged, 1)
                steps.settle()
                steps.up(dve.tensor_scalar(end_count[:, 0:1], self_ps[:, D:ROW], 1.0, None, ALU.add))
                steps.up(dve.tensor_tensor(end_y[:, 0, :], self_ps[:, 0:D], first_self[:, :], ALU.add))
                steps.settle()
                steps.up(dve.reciprocal(end_mean[:, 0:1], end_count[:, 0:1]))
                steps.settle()
                steps.up(dve.tensor_scalar(end_y[:, 0, :], end_y[:, 0, :], end_mean[:, 0:1], None, ALU.mult))
                steps.settle()
                steps.up(dve.tensor_tensor(end_y[:, 0, :], end_y[:, 0, :], first_x[:, :], ALU.add))
                end_layernorm(1, 0)
                dve.tensor_scalar(end_row[:, :], end_y[:, 0, :], end_count[:, 0:1], None, ALU.mult).then_inc(end_ready, 1)
            with dve.If(way == 0):
                steps = Count(dve, dve_end_steps)

                def dve_tile(t):
                    steps.settle()
                    wait(dve, merge_stored, t * 16)
                    steps.up(dve.tensor_copy(merge_dst[:, :], dst_sb[:, bass.ds(t, 1)]))
                    steps.up(dve.tensor_copy(merge_src[:, :], src_sb[:, bass.ds(t, 1)]))
                    steps.settle()
                    merge_start(merge_dst[:, 0:1], t + 1)
                    dve.wait_ge(tile_gathered, t * 32 + 32)
                    dve.tensor_tensor(tile_x[:, D:2 * D], tile_x[:, D:2 * D], tile_x[:, 0:D], ALU.subtract).then_inc(tile_diff, 1)
                    merge_equal(merge_dst[:, 0:1], t + 1)
                    dve.wait_ge(tile_pe, t * 7 + 7)
                    dve.tensor_tensor(tile_msg[:, 0:D], extra_ps[:, 0:D], base_row[:, 0:D], ALU.add).then_inc(tile_msg_ready, 1)
                    merge_finish(self_ps[:, 0:ROW], t + 1)

                dve_tile(0)
                start, built = steps.n, steps.built
                with dve.Fori(1, EDGE_COLS) as t:
                    steps.n = (t - 1) * MERGE_STEPS + start
                    dve_tile(t)
                assert steps.built == built + MERGE_STEPS

                steps.n = start + (EDGE_COLS - 1) * MERGE_STEPS

                def last_block(b):
                    dve.wait_ge(end_loaded, b * 32 + 32)
                    steps.settle()
                    steps.up(dve.tensor_scalar(end_count[:, :], end_sums[:, :, D], 1.0, None, ALU.max))
                    steps.settle()
                    steps.up(dve.reciprocal(end_mean[:, :], end_count[:, :]))
                    steps.settle()
                    steps.up(dve.tensor_tensor(end_y, end_sums[:, :, 0:D],
                                               end_mean[:, :].unsqueeze(2).to_broadcast([P, NPP, D]), ALU.mult))
                    steps.settle()
                    steps.up(dve.tensor_tensor(end_y, end_y, end_x[:, :, :], ALU.add))
                    end_layernorm(NPP, b)
                    dve.tensor_tensor(end_y, end_y, end_count[:, :].unsqueeze(2).to_broadcast([P, NPP, D]),
                                      ALU.mult).then_inc(end_ready, 1)
                    dve.wait_ge(end_ready, b + 1)

                last_block(0)
                start, built = steps.n, steps.built
                with dve.Fori(1, BLOCKS) as b:
                    steps.n = (b - 1) * LAST_STEPS + start
                    last_block(b)
                assert steps.built == built + LAST_STEPS, steps.built - built


_INS = ["x", "src", "dst", "L0_gnn_W1", "L0_gnn_b1", "L0_gnn_W2", "L0_gnn_b2", "L0_gnn_W3", "L0_gnn_b3",
        "L0_gnn_W4", "L0_gnn_b4"]


def kernel(**inputs):
    import numpy as np
    import concourse.bacc as bacc
    from concourse.bass_utils import run_bass_kernel_spmd

    nc = bacc.Bacc("TRN2", target_bir_lowering=False, num_devices=1)
    arrays, args = {}, []
    for name in _INS:
        a = np.ascontiguousarray(inputs[name])
        arrays[f"in_{name}"] = a
        args.append(nc.dram_tensor(f"in_{name}", a.shape, mybir.dt.from_np(a.dtype), kind="ExternalInput").ap())
    out = nc.dram_tensor("out_0", arrays["in_x"].shape, F32, kind="ExternalOutput").ap()
    gnn_program(nc, *args, out)
    r = run_bass_kernel_spmd(nc, [arrays], core_ids=[0])
    return r.results[0]["out_0"]
```
